# Optimizing a Trainium2 kernel written in Bass

```python
import numpy as np
import jax
import jax.numpy as jnp

def _softmax(x, axis=-1):
    return jax.nn.softmax(x, axis=axis)

def _gelu(x):
    return jax.nn.gelu(x, approximate=True)

def _silu(x):
    return jax.nn.silu(x)

def _sigmoid(x):
    return jax.nn.sigmoid(x)

def _layernorm(x, axis=-1, eps=1e-05):
    m = jnp.mean(x, axis=axis, keepdims=True)
    v = jnp.var(x, axis=axis, keepdims=True)
    return (x - m) / jnp.sqrt(v + eps)

def _scatter_add(tgt, idx, src, axis=0):
    return tgt.at[idx].add(src)

def _segment_sum(src, seg, n):
    return jax.ops.segment_sum(src, seg, n)
kernel_name = 'mk_dlrm_tower_d1_rec_r8_08083e'

def setup_inputs(seed: int=0):
    np.random.seed(seed)
    _w = jnp.asarray

    def _rec_inputs():
        import jax
        import jax.numpy as jnp
        _tk = jax.random.key(seed)
        dense_ctx = jax.random.normal(jax.random.fold_in(_tk, 190), (512, 16), jnp.float32)
        ids = jnp.stack([jax.random.randint(jax.random.fold_in(_tk, 200 + f), (512,), 0, v, jnp.int32) for f, v in enumerate([12500, 1000, 1000, 125000, 125000, 12500, 12500, 1250, 125000, 12500, 12500, 12500, 1250, 125000, 1250, 1000, 1000, 125000, 1000, 12500, 1000, 1250, 1250, 1000, 12500, 125000, 125000, 125000, 1250, 1000, 12500, 12500, 1000, 1000, 1250, 1250, 12500, 1000, 12500])], axis=1)
        tbl_0 = 0.05 * jax.random.normal(jax.random.fold_in(_tk, 500 + 0), (12500, 16), jnp.float32)
        tbl_1 = 0.05 * jax.random.normal(jax.random.fold_in(_tk, 500 + 1), (1000, 16), jnp.float32)
        tbl_2 = 0.05 * jax.random.normal(jax.random.fold_in(_tk, 500 + 2), (1000, 16), jnp.float32)
        tbl_3 = 0.05 * jax.random.normal(jax.random.fold_in(_tk, 500 + 3), (125000, 16), jnp.float32)
        tbl_4 = 0.05 * jax.random.normal(jax.random.fold_in(_tk, 500 + 4), (125000, 16), jnp.float32)
        tbl_5 = 0.05 * jax.random.normal(jax.random.fold_in(_tk, 500 + 5), (12500, 16), jnp.float32)
        tbl_6 = 0.05 * jax.random.normal(jax.random.fold_in(_tk, 500 + 6), (12500, 16), jnp.float32)
        tbl_7 = 0.05 * jax.random.normal(jax.random.fold_in(_tk, 500 + 7), (1250, 16), jnp.float32)
        tbl_8 = 0.05 * jax.random.normal(jax.random.fold_in(_tk, 500 + 8), (125000, 16), jnp.float32)
        tbl_9 = 0.05 * jax.random.normal(jax.random.fold_in(_tk, 500 + 9), (12500, 16), jnp.float32)
        tbl_10 = 0.05 * jax.random.normal(jax.random.fold_in(_tk, 500 + 10), (12500, 16), jnp.float32)
        tbl_11 = 0.05 * jax.random.normal(jax.random.fold_in(_tk, 500 + 11), (12500, 16), jnp.float32)
        tbl_12 = 0.05 * jax.random.normal(jax.random.fold_in(_tk, 500 + 12), (1250, 16), jnp.float32)
        tbl_13 = 0.05 * jax.random.normal(jax.random.fold_in(_tk, 500 + 13), (125000, 16), jnp.float32)
        tbl_14 = 0.05 * jax.random.normal(jax.random.fold_in(_tk, 500 + 14), (1250, 16), jnp.float32)
        tbl_15 = 0.05 * jax.random.normal(jax.random.fold_in(_tk, 500 + 15), (1000, 16), jnp.float32)
        tbl_16 = 0.05 * jax.random.normal(jax.random.fold_in(_tk, 500 + 16), (1000, 16), jnp.float32)
        tbl_17 = 0.05 * jax.random.normal(jax.random.fold_in(_tk, 500 + 17), (125000, 16), jnp.float32)
        tbl_18 = 0.05 * jax.random.normal(jax.random.fold_in(_tk, 500 + 18), (1000, 16), jnp.float32)
        tbl_19 = 0.05 * jax.random.normal(jax.random.fold_in(_tk, 500 + 19), (12500, 16), jnp.float32)
        tbl_20 = 0.05 * jax.random.normal(jax.random.fold_in(_tk, 500 + 20), (1000, 16), jnp.float32)
        tbl_21 = 0.05 * jax.random.normal(jax.random.fold_in(_tk, 500 + 21), (1250, 16), jnp.float32)
        tbl_22 = 0.05 * jax.random.normal(jax.random.fold_in(_tk, 500 + 22), (1250, 16), jnp.float32)
        tbl_23 = 0.05 * jax.random.normal(jax.random.fold_in(_tk, 500 + 23), (1000, 16), jnp.float32)
        tbl_24 = 0.05 * jax.random.normal(jax.random.fold_in(_tk, 500 + 24), (12500, 16), jnp.float32)
        tbl_25 = 0.05 * jax.random.normal(jax.random.fold_in(_tk, 500 + 25), (125000, 16), jnp.float32)
        tbl_26 = 0.05 * jax.random.normal(jax.random.fold_in(_tk, 500 + 26), (125000, 16), jnp.float32)
        tbl_27 = 0.05 * jax.random.normal(jax.random.fold_in(_tk, 500 + 27), (125000, 16), jnp.float32)
        tbl_28 = 0.05 * jax.random.normal(jax.random.fold_in(_tk, 500 + 28), (1250, 16), jnp.float32)
        tbl_29 = 0.05 * jax.random.normal(jax.random.fold_in(_tk, 500 + 29), (1000, 16), jnp.float32)
        tbl_30 = 0.05 * jax.random.normal(jax.random.fold_in(_tk, 500 + 30), (12500, 16), jnp.float32)
        tbl_31 = 0.05 * jax.random.normal(jax.random.fold_in(_tk, 500 + 31), (12500, 16), jnp.float32)
        tbl_32 = 0.05 * jax.random.normal(jax.random.fold_in(_tk, 500 + 32), (1000, 16), jnp.float32)
        tbl_33 = 0.05 * jax.random.normal(jax.random.fold_in(_tk, 500 + 33), (1000, 16), jnp.float32)
        tbl_34 = 0.05 * jax.random.normal(jax.random.fold_in(_tk, 500 + 34), (1250, 16), jnp.float32)
        tbl_35 = 0.05 * jax.random.normal(jax.random.fold_in(_tk, 500 + 35), (1250, 16), jnp.float32)
        tbl_36 = 0.05 * jax.random.normal(jax.random.fold_in(_tk, 500 + 36), (12500, 16), jnp.float32)
        tbl_37 = 0.05 * jax.random.normal(jax.random.fold_in(_tk, 500 + 37), (1000, 16), jnp.float32)
        tbl_38 = 0.05 * jax.random.normal(jax.random.fold_in(_tk, 500 + 38), (12500, 16), jnp.float32)
        _rk = jax.random.fold_in(_tk, 7)
        W_top1 = 0.0606339 * jax.random.normal(jax.random.fold_in(_tk, 801), (272, 512), jnp.float32)
        W_top2 = 0.0441942 * jax.random.normal(jax.random.fold_in(_tk, 802), (512, 256), jnp.float32)
        W_top3 = 0.0625 * jax.random.normal(jax.random.fold_in(_tk, 803), (256, 1), jnp.float32)
        b_top1 = jnp.zeros((512,), jnp.float32)
        b_top2 = jnp.zeros((256,), jnp.float32)
        return (dense_ctx, ids, tbl_0, tbl_1, tbl_2, tbl_3, tbl_4, tbl_5, tbl_6, tbl_7, tbl_8, tbl_9, tbl_10, tbl_11, tbl_12, tbl_13, tbl_14, tbl_15, tbl_16, tbl_17, tbl_18, tbl_19, tbl_20, tbl_21, tbl_22, tbl_23, tbl_24, tbl_25, tbl_26, tbl_27, tbl_28, tbl_29, tbl_30, tbl_31, tbl_32, tbl_33, tbl_34, tbl_35, tbl_36, tbl_37, tbl_38, W_top1, b_top1, W_top2, b_top2, W_top3)
    dense_ctx, ids, tbl_0, tbl_1, tbl_2, tbl_3, tbl_4, tbl_5, tbl_6, tbl_7, tbl_8, tbl_9, tbl_10, tbl_11, tbl_12, tbl_13, tbl_14, tbl_15, tbl_16, tbl_17, tbl_18, tbl_19, tbl_20, tbl_21, tbl_22, tbl_23, tbl_24, tbl_25, tbl_26, tbl_27, tbl_28, tbl_29, tbl_30, tbl_31, tbl_32, tbl_33, tbl_34, tbl_35, tbl_36, tbl_37, tbl_38, W_top1, b_top1, W_top2, b_top2, W_top3 = _rec_inputs()

    def _L0_rec_setup():
        import jax, jax.numpy as jnp
        import numpy as np
        B, M0, D = (256, 39, 16)
        CIN_SIZE = [128, 128]

        def _cin(inputs, weights):
            X0 = inputs
            Xi = inputs
            res = []
            for W in weights:
                mi = Xi.shape[1]
                z = jnp.einsum('bmd,bnd->bdmn', X0, Xi)
                z = z.reshape(z.shape[0], z.shape[1], M0 * mi)
                Xi = jnp.einsum('bdp,po->bod', z, W)
                res.append(Xi)
            res = jnp.concatenate(res, axis=1)
            return jnp.sum(res, axis=-1)
        key = jax.random.key(seed)
        k1, k2, k3 = jax.random.split(key, 3)
        inputs = jax.random.normal(k1, (B, M0, D), dtype=jnp.float32)
        W0 = jax.random.normal(k2, (M0 * M0, CIN_SIZE[0]), dtype=jnp.float32) * 0.05
        W1 = jax.random.normal(k3, (M0 * CIN_SIZE[0], CIN_SIZE[1]), dtype=jnp.float32) * 0.05
        return {'inputs': inputs, 'W0': W0, 'W1': W1}
    _L0_rec_all = _L0_rec_setup()
    _L0_rec_in = {k: v for k, v in _L0_rec_all.items() if k in ('W0', 'W1')}
    del _L0_rec_all
    return {'dense_ctx': dense_ctx, 'ids': ids, 'tbl_0': tbl_0, 'tbl_1': tbl_1, 'tbl_2': tbl_2, 'tbl_3': tbl_3, 'tbl_4': tbl_4, 'tbl_5': tbl_5, 'tbl_6': tbl_6, 'tbl_7': tbl_7, 'tbl_8': tbl_8, 'tbl_9': tbl_9, 'tbl_10': tbl_10, 'tbl_11': tbl_11, 'tbl_12': tbl_12, 'tbl_13': tbl_13, 'tbl_14': tbl_14, 'tbl_15': tbl_15, 'tbl_16': tbl_16, 'tbl_17': tbl_17, 'tbl_18': tbl_18, 'tbl_19': tbl_19, 'tbl_20': tbl_20, 'tbl_21': tbl_21, 'tbl_22': tbl_22, 'tbl_23': tbl_23, 'tbl_24': tbl_24, 'tbl_25': tbl_25, 'tbl_26': tbl_26, 'tbl_27': tbl_27, 'tbl_28': tbl_28, 'tbl_29': tbl_29, 'tbl_30': tbl_30, 'tbl_31': tbl_31, 'tbl_32': tbl_32, 'tbl_33': tbl_33, 'tbl_34': tbl_34, 'tbl_35': tbl_35, 'tbl_36': tbl_36, 'tbl_37': tbl_37, 'tbl_38': tbl_38, 'W_top1': W_top1, 'b_top1': b_top1, 'W_top2': W_top2, 'b_top2': b_top2, 'W_top3': W_top3, 'L0_rec_W0': _L0_rec_in['W0'], 'L0_rec_W1': _L0_rec_in['W1']}

def reference(dense_ctx, ids, tbl_0, tbl_1, tbl_2, tbl_3, tbl_4, tbl_5, tbl_6, tbl_7, tbl_8, tbl_9, tbl_10, tbl_11, tbl_12, tbl_13, tbl_14, tbl_15, tbl_16, tbl_17, tbl_18, tbl_19, tbl_20, tbl_21, tbl_22, tbl_23, tbl_24, tbl_25, tbl_26, tbl_27, tbl_28, tbl_29, tbl_30, tbl_31, tbl_32, tbl_33, tbl_34, tbl_35, tbl_36, tbl_37, tbl_38, W_top1, b_top1, W_top2, b_top2, W_top3, L0_rec_W0, L0_rec_W1):
    import jax
    import jax.numpy as jnp

    def _L0_rec_ref(inputs, W0, W1):
        import jax, jax.numpy as jnp
        import numpy as np
        B, M0, D = (256, 39, 16)
        CIN_SIZE = [128, 128]

        def _cin(inputs, weights):
            X0 = inputs
            Xi = inputs
            res = []
            for W in weights:
                mi = Xi.shape[1]
                z = jnp.einsum('bmd,bnd->bdmn', X0, Xi)
                z = z.reshape(z.shape[0], z.shape[1], M0 * mi)
                Xi = jnp.einsum('bdp,po->bod', z, W)
                res.append(Xi)
            res = jnp.concatenate(res, axis=1)
            return jnp.sum(res, axis=-1)
        return _cin(inputs, [W0, W1])
    e = jnp.stack([tbl_0[ids[:, 0]], tbl_1[ids[:, 1]], tbl_2[ids[:, 2]], tbl_3[ids[:, 3]], tbl_4[ids[:, 4]], tbl_5[ids[:, 5]], tbl_6[ids[:, 6]], tbl_7[ids[:, 7]], tbl_8[ids[:, 8]], tbl_9[ids[:, 9]], tbl_10[ids[:, 10]], tbl_11[ids[:, 11]], tbl_12[ids[:, 12]], tbl_13[ids[:, 13]], tbl_14[ids[:, 14]], tbl_15[ids[:, 15]], tbl_16[ids[:, 16]], tbl_17[ids[:, 17]], tbl_18[ids[:, 18]], tbl_19[ids[:, 19]], tbl_20[ids[:, 20]], tbl_21[ids[:, 21]], tbl_22[ids[:, 22]], tbl_23[ids[:, 23]], tbl_24[ids[:, 24]], tbl_25[ids[:, 25]], tbl_26[ids[:, 26]], tbl_27[ids[:, 27]], tbl_28[ids[:, 28]], tbl_29[ids[:, 29]], tbl_30[ids[:, 30]], tbl_31[ids[:, 31]], tbl_32[ids[:, 32]], tbl_33[ids[:, 33]], tbl_34[ids[:, 34]], tbl_35[ids[:, 35]], tbl_36[ids[:, 36]], tbl_37[ids[:, 37]], tbl_38[ids[:, 38]]], axis=1)
    z = _L0_rec_ref(e, L0_rec_W0, L0_rec_W1)
    z = z.reshape(z.shape[0], -1)
    h = jnp.concatenate([z, dense_ctx], axis=1)
    h = jnp.maximum(h @ W_top1 + b_top1, 0.0)
    h = jnp.maximum(h @ W_top2 + b_top2, 0.0)
    y = h @ W_top3
    return y

_drawn_inputs = setup_inputs


def setup_inputs(seed=0):
    import zlib

    import numpy as np

    out = dict(_drawn_inputs(seed))
    spreads = {'b_top1': (0.0, 0.1), 'b_top2': (0.0, 0.1)}
    factors = {'tbl_0': 4.942,
     'tbl_1': 5.101,
     'tbl_2': 4.864,
     'tbl_3': 4.873,
     'tbl_4': 5.143,
     'tbl_5': 4.903,
     'tbl_6': 5.067,
     'tbl_7': 4.871,
     'tbl_8': 5.047,
     'tbl_9': 4.518,
     'tbl_10': 5.315,
     'tbl_11': 5.006,
     'tbl_12': 4.722,
     'tbl_13': 4.46,
     'tbl_14': 4.842,
     'tbl_15': 4.922,
     'tbl_16': 5.229,
     'tbl_17': 4.786,
     'tbl_18': 5.01,
     'tbl_19': 5.135,
     'tbl_20': 5.068,
     'tbl_21': 4.809,
     'tbl_22': 4.665,
     'tbl_23': 5.066,
     'tbl_24': 4.719,
     'tbl_25': 4.984,
     'tbl_26': 5.107,
     'tbl_27': 5.217,
     'tbl_28': 4.994,
     'tbl_29': 4.974,
     'tbl_30': 4.624,
     'tbl_31': 4.531,
     'tbl_32': 5.21,
     'tbl_33': 4.817,
     'tbl_34': 5.193,
     'tbl_35': 4.868,
     'tbl_36': 4.767,
     'tbl_37': 5.013,
     'tbl_38': 5.348,
     'L0_rec_W1': 5.187}
    for name, (base, spread) in spreads.items():
        noise = np.random.default_rng([zlib.crc32(name.encode()), seed]).standard_normal(out[name].shape)
        drawn = base * np.exp(spread * noise) if base else spread * noise
        out[name] = jnp.asarray(drawn.astype(out[name].dtype))
    for name, factor in factors.items():
        out[name] = (out[name] * factor).astype(out[name].dtype)
    return out
```

```python
import numpy as np
import concourse.bass as bass
from concourse import mybir
from contextlib import ExitStack

FIELDS, DIM, BATCH, CIN = 39, 16, 512, 128
TILE = 128
TILES = BATCH // TILE
CHUNKS = 4
CB = TILE // CHUNKS
COLS = CB * DIM
SHIFTS = 3
KT = 7
ROWS = SHIFTS * FIELDS
LAST_ROWS = 2 * FIELDS
PERIODIC = ROWS + KT - 1
GB = 128 // DIM
GROUPS = CB // GB
CTX, H1, H2 = 16, 512, 256
H1T, H2T = H1 // 128, H2 // 128


def dlrm_tower(nc, tables, ids, ctx_t, w0_pq, w0_qp, w1, wt1, bt1, wt2, bt2, wt3, ident_c, diag_c, out):
    fp32, i32 = mybir.dt.float32, mybir.dt.int32
    ALU, ACT, AX = mybir.AluOpType, mybir.ActivationFunctionType, mybir.AxisListType
    ctx = ExitStack()
    with ctx:
        def sb(name, shape, dt=fp32):
            return ctx.enter_context(nc.sbuf_tensor(name, shape, dt))

        def sem(name):
            return ctx.enter_context(nc.semaphore(name))

        def sems(name, n):
            return [sem(f"{name}{i}") for i in range(n)]

        ids_sb = sb("ids_sb", [TILE, TILES, FIELDS], i32)
        emb = sb("emb", [TILE, TILES, FIELDS, DIM])
        emb_wrap = sb("emb_wrap", [TILE, PERIODIC, DIM])
        periodic = sb("periodic", [PERIODIC, CHUNKS, CB, DIM])
        left = sb("left", [ROWS, CHUNKS, CB, DIM])
        pairs = sb("pairs", [128, CHUNKS, KT, COLS])
        x1 = sb("x1", [CIN, 2, CB, DIM])
        x1_t = sb("x1_t", [128, 2, GROUPS, CIN])
        x0_diag = sb("x0_diag", [128, 2, GROUPS, FIELDS, GB])
        g_sb = sb("g_sb", [CIN, FIELDS, BATCH])
        w0_sb = sb("w0_sb", [ROWS, KT, CIN])
        wt3_sb = sb("wt3_sb", [128, H2T])
        bt1_sb = sb("bt1_sb", [128, H1T])
        bt2_sb = sb("bt2_sb", [128, H2T])
        ctx_sb = sb("ctx_sb", [CTX, BATCH])
        sum1 = sb("sum1", [CIN, BATCH])
        sum2 = sb("sum2", [CIN, BATCH])
        ident = sb("ident", [128, 128])
        diag = sb("diag", [128, GB])
        y_sb = sb("y_sb", [1, BATCH])
        spare = pairs[:, :, :, :].rearrange("p c k n -> p (c k n)")
        w1_sb = spare[:, 0:FIELDS * CIN].rearrange("p (m o) -> p m o", m=FIELDS)
        wt1_at = FIELDS * CIN
        wt1_sb = spare[:, wt1_at:wt1_at + 3 * H1].rearrange("p (k j) -> p k j", k=3)
        wt2_at = wt1_at + 3 * H1
        wt2_sb = spare[:, wt2_at:wt2_at + H1T * H2].rearrange("p (k j) -> p k j", k=H1T)
        h1, h2 = g_sb[:, 0:H1T, :], g_sb[:, H1T:H1T + H2T, :]
        w0_stage = g_sb[0:ROWS, 0:4, :].rearrange("p a b -> p (a b)")

        bank = [ctx.enter_context(nc.psum_tensor(f"bank{i}", [128, 512], fp32)) for i in range(8)]
        ps_in, ps_x1, ps_x1t, ps_x0t, ps_g = bank[0:2], bank[2:4], bank[4], bank[5], bank[6:8]

        s_ids = sem("s_ids")
        s_rows = sems("s_rows", TILES)
        s_gathered = sem("s_gathered")
        s_consts = sem("s_consts")
        s_w0 = sem("s_w0")
        s_w1, s_mlp = sem("s_w1"), sem("s_mlp")
        s_w0_sum = sem("s_w0_sum")
        s_wrap = sem("s_wrap")
        s_in_t = sems("s_in_t", 2)
        s_periodic = sems("s_periodic", 2)
        s_left = sems("s_left", CHUNKS)
        s_shift = sems("s_shift", CHUNKS)
        s_z = sems("s_z", CHUNKS)
        s_l1 = sems("s_l1", CHUNKS)
        s_x1 = sems("s_x1", 2)
        s_sum1 = sems("s_sum1", 2)
        s_xt = sem("s_xt")
        s_x1_t = sem("s_x1_t")
        s_diag = sem("s_diag")
        s_g = sems("s_g", 2)
        s_g_sb = sems("s_g_sb", 2)
        s_l2, s_sum2 = sem("s_l2"), sem("s_sum2")
        s_h1, s_h1_sb = sem("s_h1"), sem("s_h1_sb")
        s_h2, s_h2_sb = sem("s_h2"), sem("s_h2_sb")
        s_y, s_y_sb, s_out = sem("s_y"), sem("s_y_sb"), sem("s_out")

        block = ctx.enter_context(nc.Block())


        def before(t, c):
            return 2 * t + c // 2

        @block.sync
        def _(sp):
            sp.dma_start(ident[:, :], ident_c).then_inc(s_consts, 16)
            sp.dma_start(diag[:, :], diag_c).then_inc(s_consts, 16)
            half = KT * CIN
            sp.dma_start(w0_stage[:, 0:half], w0_pq).then_inc(s_w0, 16)
            sp.dma_start(w0_stage[:, half:2 * half], w0_qp).then_inc(s_w0, 16)

            def replicas(t, first):
                transposed = 2 if first else sp.to_reg(2 * t + 2)
                used = None if first else sp.to_reg(t)
                read = [None if first else sp.to_reg(CHUNKS * (t - 1) + c + 1) for c in range(CHUNKS)]
                for c in range(CHUNKS):
                    if c == 0:
                        for q in range(2):
                            sp.wait_ge(s_periodic[q], transposed)
                    if not first:
                        sp.wait_ge(s_xt, read[c])
                    for j in range(SHIFTS):
                        start = (FIELDS - KT * j) % FIELDS
                        sp.dma_start(left[j * FIELDS:(j + 1) * FIELDS, c, :, :],
                                     periodic[start:start + FIELDS, c, :, :]).then_inc(s_left[c], 16)
                    if not first:
                        sp.wait_ge(s_l1[c], used)
                    for k in range(1, KT):
                        sp.dma_start(pairs[0:ROWS, c, k, :],
                                     periodic[k:k + ROWS, c, :, :].rearrange("p b d -> p (b d)")).then_inc(s_shift[c], 16)

            replicas(0, True)
            with sp.Fori(1, TILES) as t:
                replicas(t, False)
            for c in range(CHUNKS):
                sp.wait_ge(s_l1[c], TILES)
            sp.dma_start(w1_sb, w1.rearrange("(m n) o -> n m o", n=CIN)).then_inc(s_w1, 16)
            sp.dma_start(wt1_sb[:, 0:2, :], wt1[0:2 * CIN, :].rearrange("(k p) j -> p k j", p=CIN)).then_inc(s_mlp, 16)
            sp.dma_start(wt1_sb[0:CTX, 2, :], wt1[2 * CIN:, :]).then_inc(s_mlp, 16)
            sp.dma_start(wt2_sb, wt2.rearrange("(k p) j -> p k j", p=128)).then_inc(s_mlp, 16)
            sp.dma_start(wt3_sb[:, :], wt3).then_inc(s_mlp, 16)
            sp.dma_start(bt1_sb[:, :], bt1).then_inc(s_mlp, 16)
            sp.dma_start(bt2_sb[:, :], bt2).then_inc(s_mlp, 16)
            sp.dma_start(ctx_sb[:, :], ctx_t).then_inc(s_mlp, 16)
            sp.wait_ge(s_y_sb, 1)
            sp.dma_start(out.rearrange("b o -> o b"), y_sb[:, :]).then_inc(s_out, 16)
            sp.wait_ge(s_out, 16)

        @block.gpsimd
        def _(pool):
            pool.dma_start(ids_sb[:, :, :], ids.rearrange("(t p) f -> p t f", p=TILE)).then_inc(s_ids, 16)
            pool.wait_ge(s_ids, 16)
            for t in range(TILES):
                for f in range(FIELDS):
                    pool.indirect_dma_start(
                        out=emb[:, t, f, :], out_offset=None, in_=tables[f],
                        in_offset=bass.IndirectOffsetOnAxis(ap=ids_sb[:, t, f:f + 1], axis=0),
                    ).then_inc(s_rows[t], 16)
                    if t >= 1 and f == 3:
                        pool.wait_ge(s_rows[t - 1], 16 * FIELDS)
                        pool.sem_inc(s_gathered, 1)
            pool.wait_ge(s_rows[TILES - 1], 16 * FIELDS)
            pool.sem_inc(s_gathered, 1)

        @block.vector
        def _(dve):
            def wrap(t, first):
                if first:
                    dve.wait_ge(s_rows[0], 16 * FIELDS)
                else:
                    dve.wait_ge(s_gathered, t + 1)
                    for q in range(2):
                        dve.wait_ge(s_in_t[q], 2 * t)
                src = emb[:, bass.ds(t, 1), :, :].rearrange("p a f d -> p (a f) d")
                for r in range(0, PERIODIC, FIELDS):
                    n = min(FIELDS, PERIODIC - r)
                    nc.vector.tensor_copy(emb_wrap[:, r:r + n, :], src[:, 0:n, :]).then_inc(s_wrap, 1)

            def products(t, c, first):
                dve.wait_ge(s_left[c], 16 * SHIFTS * (t + 1))
                if not first:
                    dve.wait_ge(s_l1[c], t)
                a = left[:, c, :, :].rearrange("p b d -> p (b d)")
                b = periodic[0:ROWS, c, :, :].rearrange("p b d -> p (b d)")
                nc.vector.tensor_tensor(pairs[0:ROWS, c, 0, :], a, b, ALU.mult).then_inc(s_z[c], 1)
                dve.wait_ge(s_shift[c], 16 * (KT - 1) * (t + 1))
                for k in range(1, KT):
                    z = pairs[0:ROWS, c, k, :]
                    nc.vector.tensor_tensor(z, z, a, ALU.mult).then_inc(s_z[c], 1)

            def diagonal(t, c, first):
                n = CHUNKS * t + c
                dve.wait_ge(s_xt, n + 1)
                if not first or c >= 2:
                    for q in range(2):
                        dve.wait_ge(s_g[q], 2 * (n - 1))
                src = ps_x0t[:, 0:GROUPS * FIELDS].rearrange("p (g m) -> p g m", g=GROUPS)
                nc.vector.tensor_tensor(
                    x0_diag[:, c % 2, :, :, :],
                    src[:, :, :, None].broadcast_to([128, GROUPS, FIELDS, GB]),
                    diag[:, None, None, :].broadcast_to([128, GROUPS, FIELDS, GB]), ALU.mult).then_inc(s_diag, 1)

            def sum_d(t, c):
                dve.wait_ge(s_x1[c % 2], before(t, c) + 1)
                nc.vector.tensor_reduce(sum1[:, bass.ds(t * TILE + c * CB, CB)], x1[:, c % 2, :, :], axis=AX.X,
                                        op=ALU.add).then_inc(s_sum1[c % 2], 1)

            dve.wait_ge(s_w0, 32)
            half = KT * CIN
            nc.vector.tensor_tensor(w0_sb[:, :, :].rearrange("p k o -> p (k o)"), w0_stage[:, 0:half],
                                    w0_stage[:, half:2 * half], ALU.add).then_inc(s_w0_sum, 1)
            dve.wait_ge(s_consts, 32)
            wrap(0, True)

            def tile(t, first=False, last=False):
                products(t, 0, first)
                products(t, 1, first)
                sum_d(t, 0)
                diagonal(t, 0, first)
                products(t, 2, first)
                products(t, 3, first)
                sum_d(t, 1)
                if not last:
                    wrap(t + 1, False)
                diagonal(t, 1, first)
                sum_d(t, 2)
                diagonal(t, 2, first)
                sum_d(t, 3)
                diagonal(t, 3, first)

            tile(0, first=True)
            with dve.Fori(1, TILES - 1) as t:
                tile(t)
            tile(TILES - 1, last=True)

        @block.scalar
        def _(act):
            def periodic_copy(t, q, first):
                act.wait_ge(s_in_t[q % 2], 2 * t + q // 2 + 1)
                if q == 0 and not first:
                    for c in range(CHUNKS):
                        act.wait_ge(s_left[c], 16 * SHIFTS * t)
                        act.wait_ge(s_shift[c], 16 * (KT - 1) * t)
                        act.wait_ge(s_z[c], KT * (t - 1) + 1)
                dst = periodic[:, :, :, 4 * q:4 * q + 4].rearrange("p c b d -> p d (c b)")
                src = ps_in[q % 2][0:PERIODIC, :].rearrange("p (d b) -> p d b", d=4)
                nc.scalar.copy(dst, src).then_inc(s_periodic[q % 2], 1)

            def x1_copy(t, c, first):
                s, n = c % 2, CHUNKS * t + c
                act.wait_ge(s_l1[c], t + 1)
                if not first or c >= 2:
                    act.wait_ge(s_sum1[s], before(t, c))
                    act.wait_ge(s_xt, n - 1)
                nc.scalar.copy(x1[:, s, :, :].rearrange("p b d -> p (b d)"), ps_x1[s][:, :]).then_inc(s_x1[s], 1)

            def x1_t_copy(t, c, first):
                n = CHUNKS * t + c
                act.wait_ge(s_xt, n + 1)
                if not first or c >= 2:
                    for q in range(2):
                        act.wait_ge(s_g[q], 2 * (n - 1))
                nc.scalar.copy(x1_t[:, c % 2, :, :].rearrange("p g n -> p (g n)"), ps_x1t[:, :]).then_inc(s_x1_t, 1)

            def g_copy(t, c):
                for g in range(GROUPS):
                    act.wait_ge(s_g[g % 2], 2 * (CHUNKS * t + c) + g // 2 + 1)
                    col = t * TILE + c * CB + g * GB
                    nc.scalar.copy(g_sb[:, :, bass.ds(col, GB)],
                                   ps_g[g % 2][:, 0:FIELDS * GB].rearrange("p (m b) -> p m b", b=GB)
                                   ).then_inc(s_g_sb[g % 2], 1)

            for q in range(4):
                periodic_copy(0, q, True)
            act.wait_ge(s_w0_sum, 1)

            def tile(t, first=False, last=False):
                x1_copy(t, 0, first)
                x1_copy(t, 1, first)
                x1_t_copy(t, 0, first)
                x1_copy(t, 2, first)
                x1_t_copy(t, 1, first)
                g_copy(t, 0)
                if not last:
                    for q in range(4):
                        periodic_copy(t + 1, q, False)
                x1_copy(t, 3, first)
                x1_t_copy(t, 2, first)
                g_copy(t, 1)
                x1_t_copy(t, 3, first)
                g_copy(t, 2)
                g_copy(t, 3)

            tile(0, first=True)
            with act.Fori(1, TILES - 1) as t:
                tile(t)
            tile(TILES - 1, last=True)

            act.wait_ge(s_l2, 1)
            nc.scalar.copy(sum2[:, :], bank[0][:, :]).then_inc(s_sum2, 1)
            for j in range(H1T):
                act.wait_ge(s_h1, j + 1)
                nc.scalar.activation(h1[:, j, :], bank[2 + j][:, :], ACT.Relu,
                                     bias=bt1_sb[:, j:j + 1]).then_inc(s_h1_sb, 1)
            for j in range(H2T):
                act.wait_ge(s_h2, j + 1)
                nc.scalar.activation(h2[:, j, :], bank[6 + j][:, :], ACT.Relu,
                                     bias=bt2_sb[:, j:j + 1]).then_inc(s_h2_sb, 1)
            act.wait_ge(s_y, 1)
            nc.scalar.copy(y_sb[:, :], bank[0][0:1, :]).then_inc(s_y_sb, 1)

        @block.tensor
        def _(pe):
            def inputs_t(t, first):
                pe.wait_ge(s_wrap, 4 * (t + 1))
                for q in range(4):
                    if not first or q >= 2:
                        pe.wait_ge(s_periodic[q % 2], 2 * t + q // 2)
                    for i in range(4):
                        last = nc.tensor.transpose(ps_in[q % 2][0:PERIODIC, i * TILE:(i + 1) * TILE],
                                                   emb_wrap[:, :, 4 * q + i], ident[:, :])
                    last.then_inc(s_in_t[q % 2], 1)

            def layer1(t, c, first):
                s = c % 2
                if not first or c >= 2:
                    pe.wait_ge(s_x1[s], before(t, c))
                for k in range(KT):
                    rows = ROWS if k < KT - 1 else LAST_ROWS
                    pe.wait_ge(s_z[c], KT * t + k + 1)
                    last = nc.tensor.matmul(ps_x1[s][:, :], w0_sb[0:rows, k, :], pairs[0:rows, c, k, :],
                                            start=k == 0, stop=k == KT - 1)
                last.then_inc(s_l1[c], 1)

            def chunk_t(t, c, first):
                n = CHUNKS * t + c
                pe.wait_ge(s_x1[c % 2], before(t, c) + 1)
                if not first or c >= 1:
                    pe.wait_ge(s_x1_t, n)
                    pe.wait_ge(s_diag, n)
                for g in range(GROUPS):
                    rows = slice(g * GB, (g + 1) * GB)
                    nc.tensor.transpose(ps_x1t[:, g * CIN:(g + 1) * CIN],
                                        x1[:, c % 2, rows, :].rearrange("p b d -> p (b d)"), ident[:, :])
                for g in range(GROUPS):
                    rows = slice(g * GB, (g + 1) * GB)
                    last = nc.tensor.transpose(ps_x0t[:, g * FIELDS:(g + 1) * FIELDS],
                                               left[0:FIELDS, c, rows, :].rearrange("p b d -> p (b d)"),
                                               ident[0:FIELDS, 0:FIELDS])
                last.then_inc(s_xt, 1)

            def g_products(t, c, first):
                n = CHUNKS * t + c
                pe.wait_ge(s_x1_t, n + 1)
                pe.wait_ge(s_diag, n + 1)
                for g in range(GROUPS):
                    if not first or c >= 1 or g >= 2:
                        pe.wait_ge(s_g_sb[g % 2], 2 * n + g // 2)
                    nc.tensor.matmul(ps_g[g % 2][:, 0:FIELDS * GB], x1_t[:, c % 2, g, :],
                                     x0_diag[:, c % 2, g, :, :].rearrange("p m b -> p (m b)"),
                                     start=True, stop=True).then_inc(s_g[g % 2], 1)

            pe.wait_ge(s_consts, 32)
            inputs_t(0, True)
            pe.wait_ge(s_w0_sum, 1)

            def tile(t, first=False, last=False):
                layer1(t, 0, first)
                layer1(t, 1, first)
                chunk_t(t, 0, first)
                layer1(t, 2, first)
                chunk_t(t, 1, first)
                g_products(t, 0, first)
                if not last:
                    inputs_t(t + 1, False)
                layer1(t, 3, first)
                chunk_t(t, 2, first)
                g_products(t, 1, first)
                chunk_t(t, 3, first)
                g_products(t, 2, first)
                g_products(t, 3, first)

            tile(0, first=True)
            with pe.Fori(1, TILES - 1) as t:
                tile(t)
            tile(TILES - 1, last=True)

            pe.wait_ge(s_w1, 16)
            for q in range(2):
                pe.wait_ge(s_g_sb[q], 2 * CHUNKS * TILES)
            for m in range(FIELDS):
                last = nc.tensor.matmul(bank[0][:, :], w1_sb[:, m, :], g_sb[:, m, :],
                                        start=m == 0, stop=m == FIELDS - 1)
            last.then_inc(s_l2, 1)
            pe.wait_ge(s_mlp, 16 * 7)
            for s in range(2):
                pe.wait_ge(s_sum1[s], 2 * TILES)
            for j in range(H1T):
                cols = slice(j * 128, (j + 1) * 128)
                nc.tensor.matmul(bank[2 + j][:, :], wt1_sb[:, 0, cols], sum1[:, :], start=True, stop=False)
                nc.tensor.matmul(bank[2 + j][:, :], wt1_sb[0:CTX, 2, cols], ctx_sb[:, :], start=False, stop=False)
            pe.wait_ge(s_sum2, 1)
            for j in range(H1T):
                cols = slice(j * 128, (j + 1) * 128)
                nc.tensor.matmul(bank[2 + j][:, :], wt1_sb[:, 1, cols], sum2[:, :], start=False, stop=True).then_inc(s_h1, 1)
            for j in range(H2T):
                for k in range(H1T):
                    if j == 0:
                        pe.wait_ge(s_h1_sb, k + 1)
                    last = nc.tensor.matmul(bank[6 + j][:, :], wt2_sb[:, k, j * 128:(j + 1) * 128], h1[:, k, :],
                                            start=k == 0, stop=k == H1T - 1)
                last.then_inc(s_h2, 1)
            for j in range(H2T):
                pe.wait_ge(s_h2_sb, j + 1)
                last = nc.tensor.matmul(bank[0][0:1, :], wt3_sb[:, j:j + 1], h2[:, j, :], start=j == 0, stop=j == H2T - 1)
            last.then_inc(s_y, 1)


def kernel(**inputs):
    import concourse.bacc as bacc
    from concourse.bass_utils import run_bass_kernel_spmd

    a = {k: np.ascontiguousarray(v) for k, v in inputs.items()}
    j, n, k = np.meshgrid(np.arange(SHIFTS), np.arange(FIELDS), np.arange(KT), indexing="ij")
    p, q = (n - KT * j) % FIELDS, (n + k) % FIELDS
    w0 = a["L0_rec_W0"]
    w0_pq = w0[p * FIELDS + q].reshape(ROWS, KT * CIN)
    w0_qp = np.where((p != q)[..., None], w0[q * FIELDS + p], np.float32(0)).reshape(ROWS, KT * CIN)
    arrays = {f"tbl_{f}": a[f"tbl_{f}"] for f in range(FIELDS)}
    arrays |= {
        "ids": a["ids"], "ctx_t": np.ascontiguousarray(a["dense_ctx"].T), "w0_pq": w0_pq, "w0_qp": w0_qp,
        "w1": a["L0_rec_W1"], "wt1": a["W_top1"], "bt1": np.ascontiguousarray(a["b_top1"].reshape(H1T, 128).T),
        "wt2": a["W_top2"], "bt2": np.ascontiguousarray(a["b_top2"].reshape(H2T, 128).T),
        "wt3": np.ascontiguousarray(a["W_top3"].reshape(H2T, 128).T),
        "ident_c": np.eye(128, dtype=np.float32),
        "diag_c": (np.arange(128)[:, None] // DIM == np.arange(GB)).astype(np.float32),
    }
    nc = bacc.Bacc("TRN2", target_bir_lowering=False, num_devices=1)
    aps = {name: nc.dram_tensor(name, x.shape, mybir.dt.from_np(x.dtype), kind="ExternalInput").ap()
           for name, x in arrays.items()}
    out = nc.dram_tensor("out", (BATCH, 1), mybir.dt.float32, kind="ExternalOutput").ap()
    tables = [aps.pop(f"tbl_{f}") for f in range(FIELDS)]
    dlrm_tower(nc, tables, out=out, **aps)
    r = run_bass_kernel_spmd(nc, [arrays], core_ids=[0])
    return r.results[0]["out"]
```

```python
import numpy as np
import concourse.bass as bass
from concourse import mybir
from contextlib import ExitStack

FIELDS, DIM, BATCH, CIN = 39, 16, 512, 128
TILE = 128
TILES = BATCH // TILE
CHUNKS = 4
CB = TILE // CHUNKS
COLS = CB * DIM
SHIFTS = 3
KT = 7
ROWS = SHIFTS * FIELDS
LAST_ROWS = 2 * FIELDS
PERIODIC = ROWS + KT - 1
GB = 128 // DIM
GROUPS = CB // GB
CTX, H1, H2 = 16, 512, 256
VOCAB = [12500, 1000, 1000, 125000, 125000, 12500, 12500, 1250, 125000, 12500, 12500, 12500, 1250, 125000, 1250, 1000,
         1000, 125000, 1000, 12500, 1000, 1250, 1250, 1000, 12500, 125000, 125000, 125000, 1250, 1000, 12500, 12500,
         1000, 1000, 1250, 1250, 12500, 1000, 12500]
SMALL_ROWS = 125
SMALL_VOCABS = (1000, 1250)
ORDER = sorted(range(FIELDS), key=lambda f: VOCAB[f])
OF_VOCAB = [VOCAB.count(v) for v in SMALL_VOCABS]
SMALL = sum(OF_VOCAB)
ROWS_EACH = [v // SMALL_ROWS for v in SMALL_VOCABS]
TABLE_ROWS = sum(n * r for n, r in zip(OF_VOCAB, ROWS_EACH))
VOCAB_ROWS = [slice(0, OF_VOCAB[0] * ROWS_EACH[0]), slice(OF_VOCAB[0] * ROWS_EACH[0], TABLE_ROWS)]
PARTS = 3
NEXT = 10
SMALL_BANKS = [(0, 10), (10, SMALL)]
H1T, H2T = H1 // 128, H2 // 128


def dlrm_tower(nc, tables, ids, small_ids, small_tables, row_ids, ctx_t, w0_pq, w0_qp, w1, wt1, bt1, wt2, bt2, wt3, ident_c, diag_c, out):
    fp32, i32, bf16, fp16 = mybir.dt.float32, mybir.dt.int32, mybir.dt.bfloat16, mybir.dt.float16
    ALU, ACT, AX = mybir.AluOpType, mybir.ActivationFunctionType, mybir.AxisListType
    ctx = ExitStack()
    with ctx:
        def sb(name, shape, dt=fp32):
            return ctx.enter_context(nc.sbuf_tensor(name, shape, dt))

        def sem(name):
            return ctx.enter_context(nc.semaphore(name))

        def sems(name, n):
            return [sem(f"{name}{i}") for i in range(n)]

        ids_sb = sb("ids_sb", [TILE, TILES, FIELDS], i32)
        emb = sb("emb", [TILE, TILES, FIELDS, DIM])
        emb_wrap = sb("emb_wrap", [TILE, PERIODIC, DIM])
        periodic = sb("periodic", [PERIODIC, CHUNKS, CB, DIM])
        left = sb("left", [ROWS, CHUNKS, CB, DIM])
        pairs = sb("pairs", [128, CHUNKS, KT, COLS])
        x1 = sb("x1", [CIN, 2, CB, DIM])
        x1_t = sb("x1_t", [128, 2, GROUPS, CIN])
        x0_diag = sb("x0_diag", [128, 2, GROUPS, FIELDS + 1, GB])
        g_sb = sb("g_sb", [CIN, FIELDS + 1, BATCH])
        w0_sb = sb("w0_sb", [ROWS, KT, CIN])
        wt3_sb = sb("wt3_sb", [128, H2T])
        bt1_sb = sb("bt1_sb", [128, H1T])
        bt2_sb = sb("bt2_sb", [128, H2T])
        ctx_sb = sb("ctx_sb", [CTX, BATCH])
        sum1 = g_sb[:, FIELDS, :]
        sum2 = sb("sum2", [CIN, BATCH])
        ident = sb("ident", [128, 128])
        diag = sb("diag", [128, GB])
        y_sb = sb("y_sb", [1, BATCH])
        spare = pairs[:, :, :, :].rearrange("p c k n -> p (c k n)")
        w1_sb = spare[:, 0:FIELDS * CIN].rearrange("p (m o) -> p m o", m=FIELDS)
        wt1_at = FIELDS * CIN
        wt1_sb = spare[:, wt1_at:wt1_at + 3 * H1].rearrange("p (k j) -> p k j", k=3)
        wt2_at = wt1_at + 3 * H1
        wt2_sb = spare[:, wt2_at:wt2_at + H1T * H2].rearrange("p (k j) -> p k j", k=H1T)
        h1, h2 = g_sb[:, 0:H1T, :], g_sb[:, H1T:H1T + H2T, :]
        stage = g_sb[:, :, :].rearrange("p m b -> p (m b)")
        w0_stage = stage[0:ROWS, 0:2 * KT * CIN]
        at = 2 * KT * CIN
        table = stage[:, at:at + TABLE_ROWS * DIM].rearrange("p (r d) -> p r d", d=DIM)
        at += TABLE_ROWS * DIM
        parts = stage[:, at:at + TABLE_ROWS * DIM * PARTS // 2].bitcast(bf16).rearrange("p (r n d) -> p r n d", n=PARTS, d=DIM)
        at += TABLE_ROWS * DIM * PARTS // 2
        ids_all = stage[:, at:at + (SMALL + NEXT) * TILE].bitcast(i32)
        at += (SMALL + NEXT) * TILE
        ids_16 = stage[:, at:at + (SMALL + NEXT) * TILE // 2].bitcast(fp16)
        at += (SMALL + NEXT) * TILE // 2
        rest = stage[:, at:at + TABLE_ROWS * DIM].rearrange("p (r d) -> p r d", d=DIM)
        one_hot_next = stage[:, at:at + NEXT * ROWS_EACH[0] * TILE // 2].bitcast(bf16).rearrange("p (r b) -> p r b", b=TILE)
        one_hot = spare[:, 0:TABLE_ROWS * TILE // 2].bitcast(bf16).rearrange("p (r b) -> p r b", b=TILE)
        row_of = sb("row_of", [128, len(SMALL_VOCABS), max(ROWS_EACH)])

        bank = [ctx.enter_context(nc.psum_tensor(f"bank{i}", [128, 512], fp32)) for i in range(8)]
        ps_in, ps_x1, ps_x1t, ps_x0t, ps_g = bank[0:2], bank[2:4], bank[4], bank[5], bank[6:8]

        s_ids = sem("s_ids")
        s_small_ids = sem("s_small_ids")
        s_tables = sems("s_tables", len(SMALL_VOCABS))
        s_next_ids = sem("s_next_ids")
        s_ids_16 = sem("s_ids_16")
        s_parts = sems("s_parts", len(SMALL_VOCABS))
        s_one_hot = sems("s_one_hot", len(SMALL_VOCABS))
        s_one_hot_next = sem("s_one_hot_next")
        s_picked = sems("s_picked", 3)
        s_small = sem("s_small")
        s_ones = sem("s_ones")
        s_rows = sems("s_rows", TILES)
        s_gathered = sem("s_gathered")
        s_consts = sem("s_consts")
        s_w0 = sem("s_w0")
        s_w1, s_mlp = sem("s_w1"), sem("s_mlp")
        s_w0_sum = sem("s_w0_sum")
        s_wrap = sem("s_wrap")
        s_in_t = sems("s_in_t", 2)
        s_periodic = sems("s_periodic", 2)
        s_left = sems("s_left", CHUNKS)
        s_shift = [sems(f"s_shift{c}_", KT) for c in range(CHUNKS)]
        s_z = sems("s_z", CHUNKS)
        s_l1 = sems("s_l1", CHUNKS)
        s_x1 = sems("s_x1", 2)
        s_xt = sem("s_xt")
        s_x1_t = sem("s_x1_t")
        s_diag = sem("s_diag")
        s_g = sems("s_g", 2)
        s_g_sb = sems("s_g_sb", 2)
        s_l2, s_sum2 = sem("s_l2"), sem("s_sum2")
        s_h1, s_h1_sb = sem("s_h1"), sem("s_h1_sb")
        s_h2, s_h2_sb = sem("s_h2"), sem("s_h2_sb")
        s_y, s_y_sb, s_out = sem("s_y"), sem("s_y_sb"), sem("s_out")

        block = ctx.enter_context(nc.Block())


        def before(t, c):
            return 2 * t + c // 2

        def gathered_from(t):
            return (SMALL, NEXT)[t] if t < 2 else 0

        @block.sync
        def _(sp):
            sp.dma_start(ids_sb[:, :, :], ids.rearrange("(t p) f -> p t f", p=TILE)).then_inc(s_ids, 16)
            sp.dma_start(row_of[:, :, :], row_ids).then_inc(s_small_ids, 16)
            mine = SMALL * TILE
            sp.dma_start(ids_all[:, 0:mine], small_ids[:, 0:mine].broadcast_to([128, mine])).then_inc(s_small_ids, 16)
            for v, rows in enumerate(VOCAB_ROWS):
                sp.dma_start(table[:, rows, :], small_tables.rearrange("p (r d) -> p r d", d=DIM)[:, rows, :]).then_inc(s_tables[v], 16)
            sp.dma_start(ids_all[:, mine:], small_ids[:, mine:].broadcast_to([128, NEXT * TILE])).then_inc(s_next_ids, 16)
            sp.dma_start(ident[:, :], ident_c).then_inc(s_consts, 16)
            sp.dma_start(diag[:, :], diag_c).then_inc(s_consts, 16)
            half = KT * CIN
            sp.dma_start(w0_stage[:, 0:half], w0_pq).then_inc(s_w0, 16)
            sp.dma_start(w0_stage[:, half:2 * half], w0_qp).then_inc(s_w0, 16)

            def replicas(t, first):
                transposed = 2 if first else sp.to_reg(2 * t + 2)
                used = None if first else sp.to_reg(t)
                read = [None if first else sp.to_reg(CHUNKS * (t - 1) + c + 1) for c in range(CHUNKS)]
                for c in range(CHUNKS):
                    if c == 0:
                        for q in range(2):
                            sp.wait_ge(s_periodic[q], transposed)
                    if not first:
                        sp.wait_ge(s_xt, read[c])
                    for j in range(SHIFTS):
                        start = (FIELDS - KT * j) % FIELDS
                        sp.dma_start(left[j * FIELDS:(j + 1) * FIELDS, c, :, :],
                                     periodic[start:start + FIELDS, c, :, :]).then_inc(s_left[c], 16)
                    if not first:
                        sp.wait_ge(s_l1[c], used)
                    for k in range(1, KT):
                        sp.dma_start(pairs[0:ROWS, c, k, :],
                                     periodic[k:k + ROWS, c, :, :].rearrange("p b d -> p (b d)")).then_inc(s_shift[c][k], 16)

            replicas(0, True)
            with sp.Fori(1, TILES) as t:
                replicas(t, False)
            for c in range(CHUNKS):
                sp.wait_ge(s_l1[c], TILES)
            sp.dma_start(w1_sb, w1.rearrange("(m n) o -> n m o", n=CIN)).then_inc(s_w1, 16)
            sp.dma_start(wt1_sb[:, 0:2, :], wt1[0:2 * CIN, :].rearrange("(k p) j -> p k j", p=CIN)).then_inc(s_mlp, 16)
            sp.dma_start(wt1_sb[0:CTX, 2, :], wt1[2 * CIN:, :]).then_inc(s_mlp, 16)
            sp.dma_start(wt2_sb, wt2.rearrange("(k p) j -> p k j", p=128)).then_inc(s_mlp, 16)
            sp.dma_start(wt3_sb[:, :], wt3).then_inc(s_mlp, 16)
            sp.dma_start(bt1_sb[:, :], bt1).then_inc(s_mlp, 16)
            sp.dma_start(bt2_sb[:, :], bt2).then_inc(s_mlp, 16)
            sp.dma_start(ctx_sb[:, :], ctx_t).then_inc(s_mlp, 16)
            sp.wait_ge(s_y_sb, 1)
            sp.dma_start(out.rearrange("b o -> o b"), y_sb[:, :]).then_inc(s_out, 16)
            sp.wait_ge(s_out, 16)

        @block.gpsimd
        def _(pool):
            pool.wait_ge(s_ids, 16)
            for t in range(TILES):
                for f in range(gathered_from(t), FIELDS):
                    pool.indirect_dma_start(
                        out=emb[:, t, f, :], out_offset=None, in_=tables[f],
                        in_offset=bass.IndirectOffsetOnAxis(ap=ids_sb[:, t, f:f + 1], axis=0),
                    ).then_inc(s_rows[t], 16)
                    if t >= 2 and f == 3:
                        pool.wait_ge(s_rows[t - 1], 16 * (FIELDS - gathered_from(t - 1)))
                        pool.sem_inc(s_gathered, 1)
            pool.wait_ge(s_rows[TILES - 1], 16 * FIELDS)
            pool.sem_inc(s_gathered, 1)

        @block.vector
        def _(dve):
            def wrap(t, first):
                src = emb[:, bass.ds(t, 1), :, :].rearrange("p a f d -> p (a f) d")
                dve.wait_ge(s_small, 2 if first else 3)
                if not first:
                    dve.wait_ge(s_gathered, t)
                    for q in range(2):
                        dve.wait_ge(s_in_t[q], 2 * t)
                ready = SMALL if first else FIELDS
                for r in range(0, PERIODIC, FIELDS):
                    n = min(ready, PERIODIC - r)
                    nc.vector.tensor_copy(emb_wrap[:, r:r + n, :], src[:, 0:n, :]).then_inc(s_wrap, 1)
                if first:
                    dve.wait_ge(s_rows[0], 16 * (FIELDS - SMALL))
                    for r in range(0, ROWS, FIELDS):
                        nc.vector.tensor_copy(emb_wrap[:, r + SMALL:r + FIELDS, :], src[:, SMALL:, :]).then_inc(s_wrap, 1)

            def products(t, c, first):
                dve.wait_ge(s_left[c], 16 * SHIFTS * (t + 1))
                if not first:
                    dve.wait_ge(s_l1[c], t)
                a = left[:, c, :, :].rearrange("p b d -> p (b d)")
                b = periodic[0:ROWS, c, :, :].rearrange("p b d -> p (b d)")
                nc.vector.tensor_tensor(pairs[0:ROWS, c, 0, :], a, b, ALU.mult).then_inc(s_z[c], 1)
                for k in range(1, KT):
                    dve.wait_ge(s_shift[c][k], 16 * (t + 1))
                    z = pairs[0:ROWS, c, k, :]
                    nc.vector.tensor_tensor(z, z, a, ALU.mult).then_inc(s_z[c], 1)

            def diagonal(t, c, first):
                n = CHUNKS * t + c
                dve.wait_ge(s_xt, n + 1)
                if not first or c >= 2:
                    for q in range(2):
                        dve.wait_ge(s_g[q], 2 * (n - 1))
                src = ps_x0t[:, 0:GROUPS * FIELDS].rearrange("p (g m) -> p g m", g=GROUPS)
                nc.vector.tensor_tensor(
                    x0_diag[:, c % 2, :, 0:FIELDS, :],
                    src[:, :, :, None].broadcast_to([128, GROUPS, FIELDS, GB]),
                    diag[:, None, None, :].broadcast_to([128, GROUPS, FIELDS, GB]), ALU.mult).then_inc(s_diag, 1)

            dve.wait_ge(s_small_ids, 32)
            mine = SMALL * TILE
            nc.vector.tensor_copy(ids_16[:, 0:mine], ids_all[:, 0:mine]).then_inc(s_ids_16, 1)
            dve.wait_ge(s_ids_16, 1)
            def compares(v):
                f0, rows = sum(OF_VOCAB[:v]), VOCAB_ROWS[v].start
                for r in range(ROWS_EACH[v]):
                    n = OF_VOCAB[v]
                    nc.vector.tensor_scalar(
                        one_hot[:, rows + r * n:rows + (r + 1) * n, :].rearrange("p f b -> p (f b)"),
                        ids_16[:, f0 * TILE:(f0 + n) * TILE], row_of[:, v, r:r + 1], None,
                        ALU.is_equal).then_inc(s_one_hot[v], 1)

            def subtract_part(v, n):
                rows = VOCAB_ROWS[v]
                src, dst = (table[:, rows, :], rest[:, rows, :]) if n == 0 else (rest[:, rows, :], parts[:, rows, 2, :])
                dve.wait_ge(s_parts[v], 2 * n + 1)
                nc.vector.tensor_tensor(dst, src, parts[:, rows, n, :], ALU.subtract).then_inc(s_parts[v], 1)

            def sum_parts(q):
                dve.wait_ge(s_picked[q], 1)
                t, (f0, f1), picked = (0, SMALL_BANKS[q], ps_in[q]) if q < 2 else (1, (0, NEXT), ps_g[0])
                nc.vector.tensor_reduce(
                    emb[:, t, f0:f1, :],
                    picked[:, 0:(f1 - f0) * PARTS * DIM].rearrange("p (f n d) -> p f d n", n=PARTS, d=DIM),
                    axis=AX.X, op=ALU.add).then_inc(s_small, 1)

            compares(0)
            subtract_part(0, 0)
            subtract_part(1, 0)
            subtract_part(0, 1)
            compares(1)
            subtract_part(1, 1)
            sum_parts(0)
            dve.wait_ge(s_w0, 32)
            half = KT * CIN
            nc.vector.tensor_tensor(w0_sb[:, :, :].rearrange("p k o -> p (k o)"), w0_stage[:, 0:half],
                                    w0_stage[:, half:2 * half], ALU.add).then_inc(s_w0_sum, 1)
            dve.wait_ge(s_consts, 32)
            for s in range(2):
                nc.vector.tensor_copy(x0_diag[:, s, :, FIELDS, :],
                                      diag[:, None, :].broadcast_to([128, GROUPS, GB])).then_inc(s_ones, 1)
            dve.wait_ge(s_next_ids, 16)
            nc.vector.tensor_copy(ids_16[:, mine:], ids_all[:, mine:]).then_inc(s_ids_16, 1)
            sum_parts(1)
            wrap(0, True)
            dve.wait_ge(s_ids_16, 2)
            for v in range(2):
                dve.wait_ge(s_parts[v], 4)
            for r in range(ROWS_EACH[0]):
                nc.vector.tensor_scalar(
                    one_hot_next[:, r * NEXT:(r + 1) * NEXT, :].rearrange("p f b -> p (f b)"),
                    ids_16[:, mine:], row_of[:, 0, r:r + 1], None, ALU.is_equal).then_inc(s_one_hot_next, 1)
            sum_parts(2)

            def tile(t, first=False, last=False):
                products(t, 0, first)
                products(t, 1, first)
                products(t, 2, first)
                diagonal(t, 0, first)
                products(t, 3, first)
                if not last:
                    wrap(t + 1, False)
                diagonal(t, 1, first)
                diagonal(t, 2, first)
                diagonal(t, 3, first)

            tile(0, first=True)
            with dve.Fori(1, TILES - 1) as t:
                tile(t)
            tile(TILES - 1, last=True)

        @block.scalar
        def _(act):
            def periodic_copy(t, q, first):
                act.wait_ge(s_in_t[q % 2], 2 * t + q // 2 + 1)
                if q == 0 and not first:
                    for c in range(CHUNKS):
                        act.wait_ge(s_z[c], KT * t)
                dst = periodic[:, :, :, 4 * q:4 * q + 4].rearrange("p c b d -> p d (c b)")
                src = ps_in[q % 2][0:PERIODIC, :].rearrange("p (d b) -> p d b", d=4)
                nc.scalar.copy(dst, src).then_inc(s_periodic[q % 2], 1)

            def x1_copy(t, c, first):
                s, n = c % 2, CHUNKS * t + c
                act.wait_ge(s_l1[c], t + 1)
                if not first or c >= 2:
                    act.wait_ge(s_xt, n - 1)
                nc.scalar.copy(x1[:, s, :, :].rearrange("p b d -> p (b d)"), ps_x1[s][:, :]).then_inc(s_x1[s], 1)

            def x1_t_copy(t, c, first):
                n = CHUNKS * t + c
                act.wait_ge(s_xt, n + 1)
                if not first or c >= 2:
                    for q in range(2):
                        act.wait_ge(s_g[q], 2 * (n - 1))
                nc.scalar.copy(x1_t[:, c % 2, :, :].rearrange("p g n -> p (g n)"), ps_x1t[:, :]).then_inc(s_x1_t, 1)

            def g_copy(t, c):
                for g in range(GROUPS):
                    act.wait_ge(s_g[g % 2], 2 * (CHUNKS * t + c) + g // 2 + 1)
                    col = t * TILE + c * CB + g * GB
                    nc.scalar.copy(g_sb[:, :, bass.ds(col, GB)],
                                   ps_g[g % 2][:, 0:(FIELDS + 1) * GB].rearrange("p (m b) -> p m b", b=GB)
                                   ).then_inc(s_g_sb[g % 2], 1)

            for n, src in enumerate((table, rest)):
                for v, rows in enumerate(VOCAB_ROWS):
                    if n == 0:
                        act.wait_ge(s_tables[v], 16)
                    else:
                        act.wait_ge(s_parts[v], 2)
                    nc.scalar.copy(parts[:, rows, n, :], src[:, rows, :]).then_inc(s_parts[v], 1)
            for q in range(4):
                periodic_copy(0, q, True)
            act.wait_ge(s_w0_sum, 1)

            def tile(t, first=False, last=False):
                x1_copy(t, 0, first)
                x1_copy(t, 1, first)
                x1_t_copy(t, 0, first)
                x1_copy(t, 2, first)
                x1_t_copy(t, 1, first)
                g_copy(t, 0)
                if not last:
                    for q in range(4):
                        periodic_copy(t + 1, q, False)
                x1_copy(t, 3, first)
                x1_t_copy(t, 2, first)
                g_copy(t, 1)
                x1_t_copy(t, 3, first)
                g_copy(t, 2)
                g_copy(t, 3)

            tile(0, first=True)
            with act.Fori(1, TILES - 1) as t:
                tile(t)
            tile(TILES - 1, last=True)

            act.wait_ge(s_l2, 1)
            nc.scalar.copy(sum2[:, :], bank[0][:, :]).then_inc(s_sum2, 1)
            for j in range(H1T):
                act.wait_ge(s_h1, j + 1)
                nc.scalar.activation(h1[:, j, :], bank[2 + j][:, :], ACT.Relu,
                                     bias=bt1_sb[:, j:j + 1]).then_inc(s_h1_sb, 1)
            for j in range(H2T):
                act.wait_ge(s_h2, j + 1)
                nc.scalar.activation(h2[:, j, :], bank[6 + j][:, :], ACT.Relu,
                                     bias=bt2_sb[:, j:j + 1]).then_inc(s_h2_sb, 1)
            act.wait_ge(s_y, 1)
            nc.scalar.copy(y_sb[:, :], bank[0][0:1, :]).then_inc(s_y_sb, 1)

        @block.tensor
        def _(pe):
            def inputs_t(t, first):
                pe.wait_ge(s_wrap, 4 * t + 7)
                for q in range(4):
                    if not first or q >= 2:
                        pe.wait_ge(s_periodic[q % 2], 2 * t + q // 2)
                    for i in range(4):
                        last = nc.tensor.transpose(ps_in[q % 2][0:PERIODIC, i * TILE:(i + 1) * TILE],
                                                   emb_wrap[:, :, 4 * q + i], ident[:, :])
                    last.then_inc(s_in_t[q % 2], 1)

            def layer1(t, c, first):
                s = c % 2
                if not first or c >= 2:
                    pe.wait_ge(s_x1[s], before(t, c))
                for k in range(KT):
                    rows = ROWS if k < KT - 1 else LAST_ROWS
                    pe.wait_ge(s_z[c], KT * t + k + 1)
                    last = nc.tensor.matmul(ps_x1[s][:, :], w0_sb[0:rows, k, :], pairs[0:rows, c, k, :],
                                            start=k == 0, stop=k == KT - 1)
                last.then_inc(s_l1[c], 1)

            def chunk_t(t, c, first):
                n = CHUNKS * t + c
                pe.wait_ge(s_x1[c % 2], before(t, c) + 1)
                if not first or c >= 1:
                    pe.wait_ge(s_x1_t, n)
                    pe.wait_ge(s_diag, n)
                for g in range(GROUPS):
                    rows = slice(g * GB, (g + 1) * GB)
                    nc.tensor.transpose(ps_x1t[:, g * CIN:(g + 1) * CIN],
                                        x1[:, c % 2, rows, :].rearrange("p b d -> p (b d)"), ident[:, :])
                for g in range(GROUPS):
                    rows = slice(g * GB, (g + 1) * GB)
                    last = nc.tensor.transpose(ps_x0t[:, g * FIELDS:(g + 1) * FIELDS],
                                               left[0:FIELDS, c, rows, :].rearrange("p b d -> p (b d)"),
                                               ident[0:FIELDS, 0:FIELDS])
                last.then_inc(s_xt, 1)

            def g_products(t, c, first):
                n = CHUNKS * t + c
                pe.wait_ge(s_x1_t, n + 1)
                pe.wait_ge(s_diag, n + 1)
                for g in range(GROUPS):
                    if not first or c >= 1 or g >= 2:
                        pe.wait_ge(s_g_sb[g % 2], 2 * n + g // 2)
                    nc.tensor.matmul(ps_g[g % 2][:, 0:(FIELDS + 1) * GB], x1_t[:, c % 2, g, :],
                                     x0_diag[:, c % 2, g, :, :].rearrange("p m b -> p (m b)"),
                                     start=True, stop=True).then_inc(s_g[g % 2], 1)

            f = 0
            for v, (fields, rows) in enumerate(zip(OF_VOCAB, ROWS_EACH)):
                pe.wait_ge(s_one_hot[v], rows)
                pe.wait_ge(s_parts[v], 4)
                for i in range(fields):
                    q = int(f >= SMALL_BANKS[1][0])
                    at = (f - SMALL_BANKS[q][0]) * PARTS * DIM
                    for r in range(rows):
                        last = nc.tensor.matmul(ps_in[q][:, at:at + PARTS * DIM],
                                                one_hot[:, VOCAB_ROWS[v].start + r * fields + i, :],
                                                parts[:, VOCAB_ROWS[v].start + i * rows + r, :, :].rearrange("p n d -> p (n d)"),
                                                start=r == 0, stop=r == rows - 1)
                    f += 1
                    if f == SMALL_BANKS[q][1]:
                        last.then_inc(s_picked[q], 1)
            pe.wait_ge(s_consts, 32)
            inputs_t(0, True)
            pe.wait_ge(s_one_hot_next, ROWS_EACH[0])
            for i in range(NEXT):
                for r in range(ROWS_EACH[0]):
                    last = nc.tensor.matmul(ps_g[0][:, i * PARTS * DIM:(i + 1) * PARTS * DIM],
                                            one_hot_next[:, r * NEXT + i, :],
                                            parts[:, i * ROWS_EACH[0] + r, :, :].rearrange("p n d -> p (n d)"),
                                            start=r == 0, stop=r == ROWS_EACH[0] - 1)
            last.then_inc(s_picked[2], 1)
            pe.wait_ge(s_w0_sum, 1)
            pe.wait_ge(s_ones, 2)

            def tile(t, first=False, last=False):
                layer1(t, 0, first)
                layer1(t, 1, first)
                chunk_t(t, 0, first)
                layer1(t, 2, first)
                chunk_t(t, 1, first)
                g_products(t, 0, first)
                if not last:
                    inputs_t(t + 1, False)
                layer1(t, 3, first)
                chunk_t(t, 2, first)
                g_products(t, 1, first)
                chunk_t(t, 3, first)
                g_products(t, 2, first)
                g_products(t, 3, first)

            tile(0, first=True)
            with pe.Fori(1, TILES - 1) as t:
                tile(t)
            tile(TILES - 1, last=True)

            pe.wait_ge(s_w1, 16)
            for q in range(2):
                pe.wait_ge(s_g_sb[q], 2 * CHUNKS * TILES)
            for m in range(FIELDS):
                last = nc.tensor.matmul(bank[0][:, :], w1_sb[:, m, :], g_sb[:, m, :],
                                        start=m == 0, stop=m == FIELDS - 1)
            last.then_inc(s_l2, 1)
            pe.wait_ge(s_mlp, 16 * 7)
            for j in range(H1T):
                cols = slice(j * 128, (j + 1) * 128)
                nc.tensor.matmul(bank[2 + j][:, :], wt1_sb[:, 0, cols], sum1, start=True, stop=False)
                nc.tensor.matmul(bank[2 + j][:, :], wt1_sb[0:CTX, 2, cols], ctx_sb[:, :], start=False, stop=False)
            pe.wait_ge(s_sum2, 1)
            for j in range(H1T):
                cols = slice(j * 128, (j + 1) * 128)
                nc.tensor.matmul(bank[2 + j][:, :], wt1_sb[:, 1, cols], sum2[:, :], start=False, stop=True).then_inc(s_h1, 1)
            for j in range(H2T):
                for k in range(H1T):
                    if j == 0:
                        pe.wait_ge(s_h1_sb, k + 1)
                    last = nc.tensor.matmul(bank[6 + j][:, :], wt2_sb[:, k, j * 128:(j + 1) * 128], h1[:, k, :],
                                            start=k == 0, stop=k == H1T - 1)
                last.then_inc(s_h2, 1)
            for j in range(H2T):
                pe.wait_ge(s_h2_sb, j + 1)
                last = nc.tensor.matmul(bank[0][0:1, :], wt3_sb[:, j:j + 1], h2[:, j, :], start=j == 0, stop=j == H2T - 1)
            last.then_inc(s_y, 1)


def kernel(**inputs):
    import concourse.bacc as bacc
    from concourse.bass_utils import run_bass_kernel_spmd

    a = {k: np.ascontiguousarray(v) for k, v in inputs.items()}
    order = np.array(ORDER)
    small = [a[f"tbl_{f}"].reshape(SMALL_ROWS, -1) for f in ORDER[:SMALL]]
    small_tables = np.zeros((128, TABLE_ROWS * DIM), np.float32)
    small_tables[:SMALL_ROWS] = np.concatenate(small, axis=1)
    r = np.arange(max(ROWS_EACH))
    row_ids = np.stack([np.arange(128)[:, None] * n + r for n in ROWS_EACH], axis=1).astype(np.float32)
    j, n, k = np.meshgrid(np.arange(SHIFTS), np.arange(FIELDS), np.arange(KT), indexing="ij")
    p, q = (n - KT * j) % FIELDS, (n + k) % FIELDS
    w0 = a["L0_rec_W0"]
    p, q = order[p], order[q]
    w0_pq = w0[p * FIELDS + q].reshape(ROWS, KT * CIN)
    w0_qp = np.where((p != q)[..., None], w0[q * FIELDS + p], np.float32(0)).reshape(ROWS, KT * CIN)
    arrays = {f"tbl_{f}": a[f"tbl_{f}"] for f in range(FIELDS)}
    w1 = a["L0_rec_W1"].reshape(FIELDS, CIN, CIN)[order].reshape(FIELDS * CIN, CIN)
    ids = np.ascontiguousarray(a["ids"][:, order])
    arrays |= {
        "ids": ids, "small_ids": np.concatenate([ids[:TILE, :SMALL].T, ids[TILE:2 * TILE, :NEXT].T]).reshape(1, -1),
        "small_tables": small_tables, "row_ids": row_ids, "ctx_t": np.ascontiguousarray(a["dense_ctx"].T), "w0_pq": w0_pq, "w0_qp": w0_qp,
        "w1": w1, "wt1": a["W_top1"], "bt1": np.ascontiguousarray(a["b_top1"].reshape(H1T, 128).T),
        "wt2": a["W_top2"], "bt2": np.ascontiguousarray(a["b_top2"].reshape(H2T, 128).T),
        "wt3": np.ascontiguousarray(a["W_top3"].reshape(H2T, 128).T),
        "ident_c": np.eye(128, dtype=np.float32),
        "diag_c": (np.arange(128)[:, None] // DIM == np.arange(GB)).astype(np.float32),
    }
    nc = bacc.Bacc("TRN2", target_bir_lowering=False, num_devices=1)
    aps = {name: nc.dram_tensor(name, x.shape, mybir.dt.from_np(x.dtype), kind="ExternalInput").ap()
           for name, x in arrays.items()}
    out = nc.dram_tensor("out", (BATCH, 1), mybir.dt.float32, kind="ExternalOutput").ap()
    tables = [aps.pop(f"tbl_{f}") for f in ORDER]
    dlrm_tower(nc, tables, out=out, **aps)
    r = run_bass_kernel_spmd(nc, [arrays], core_ids=[0])
    return r.results[0]["out"]
```

```python
import numpy as np
import concourse.bass as bass
from concourse import mybir
from contextlib import ExitStack

FIELDS, DIM, BATCH, CIN = 39, 16, 512, 128
TILE = 128
TILES = BATCH // TILE
CHUNKS = 4
CB = TILE // CHUNKS
COLS = CB * DIM
SHIFTS = 3
KT = 7
SPLIT = [3, 4, 5]
WHOLE = [k for k in range(KT) if k not in SPLIT]
ROWS = SHIFTS * FIELDS
LAST_ROWS = 2 * FIELDS
PERIODIC = ROWS + KT - 1
GB = 128 // DIM
GROUPS = CB // GB
QUARTERS = 4
LATE = 30
WRAPS = 7
CTX, H1, H2 = 16, 512, 256
VOCAB = [12500, 1000, 1000, 125000, 125000, 12500, 12500, 1250, 125000, 12500, 12500, 12500, 1250, 125000, 1250, 1000,
         1000, 125000, 1000, 12500, 1000, 1250, 1250, 1000, 12500, 125000, 125000, 125000, 1250, 1000, 12500, 12500,
         1000, 1000, 1250, 1250, 12500, 1000, 12500]
SMALL_ROWS = 125
SMALL_VOCABS = (1000, 1250)
ORDER = sorted(range(FIELDS), key=lambda f: VOCAB[f])
OF_VOCAB = [VOCAB.count(v) for v in SMALL_VOCABS]
SMALL = sum(OF_VOCAB)
ROWS_EACH = [v // SMALL_ROWS for v in SMALL_VOCABS]
TABLE_ROWS = sum(n * r for n, r in zip(OF_VOCAB, ROWS_EACH))
VOCAB_ROWS = [slice(0, OF_VOCAB[0] * ROWS_EACH[0]), slice(OF_VOCAB[0] * ROWS_EACH[0], TABLE_ROWS)]
PARTS = 3
ONE_HOT_TILES = 2
PICKED = [(t, f, g) for t in range(ONE_HOT_TILES) for f, g in ((0, 10), (10, SMALL))]
L2_WHOLE = 13
L2_SPLIT = FIELDS - L2_WHOLE
W1_FIRST = KT * COLS // CIN
H1T, H2T = H1 // 128, H2 // 128


def dlrm_tower(nc, tables, ids, small_ids, small_tables, row_ids, ctx_t, w0_pq, w0_qp, w1, wt1, bt1, wt2, bt2, wt3,
               ident_c, diag_c, out):
    fp32, i32, bf16, fp16 = mybir.dt.float32, mybir.dt.int32, mybir.dt.bfloat16, mybir.dt.float16
    fp32r = mybir.dt.float32r
    ALU, ACT, AX = mybir.AluOpType, mybir.ActivationFunctionType, mybir.AxisListType
    ctx = ExitStack()
    with ctx:
        def sb(name, shape, dt=fp32):
            return ctx.enter_context(nc.sbuf_tensor(name, shape, dt))

        def next_at():
            return -(-nc.sbuf_base // 32) * 32

        def sb_over(name, tensor_at, shape, dt):
            return nc.alloc_sbuf_tensor_at(name, shape, dt, offset=tensor_at)

        def sem(name):
            return ctx.enter_context(nc.semaphore(name))

        def sems(name, n):
            return [sem(f"{name}{i}") for i in range(n)]

        ids_sb = sb("ids_sb", [TILE, TILES, FIELDS], i32)
        emb_at = next_at()
        emb = sb("emb", [TILE, TILES, FIELDS, DIM])
        emb_wrap = sb("emb_wrap", [TILE, PERIODIC, DIM])
        periodic_at = next_at()
        periodic = sb("periodic", [PERIODIC, CHUNKS, CB, DIM])
        left = sb("left", [128, CHUNKS, CB, DIM])
        pairs_at = next_at()
        pairs = sb("pairs", [128, CHUNKS, KT, COLS])
        z_high = sb("z_high", [ROWS, len(SPLIT), COLS], fp32r)
        z_low = sb_over("z_low", pairs_at, [128, CHUNKS, KT, COLS], fp32r)
        x1 = sb("x1", [CIN, 2, CB, DIM])
        x1_t = sb("x1_t", [128, 2, GROUPS, CIN])
        x0_diag = sb("x0_diag", [128, 2, GROUPS, FIELDS + 1, GB])
        w0_at = next_at()
        w0_sb = sb("w0_sb", [ROWS, KT, CIN])
        w0_high = sb("w0_high", [ROWS, len(SPLIT), CIN], fp32r)
        w0_low = sb_over("w0_low", w0_at, [ROWS, KT, CIN], fp32r)
        g_at = next_at()
        g_sb = sb("g_sb", [CIN, FIELDS + 1, BATCH])
        wt3_sb = sb("wt3_sb", [128, H2T])
        bt1_sb = sb("bt1_sb", [128, H1T])
        bt2_sb = sb("bt2_sb", [128, H2T])
        ctx_part = sb("ctx_part", [128, H1T, BATCH])
        sum1 = g_sb[:, FIELDS, :]
        flat = emb_wrap[:, :, :].rearrange("p f d -> p (f d)")
        y_sb = flat[0:1, 0:BATCH]
        ident = sb("ident", [128, 128])
        diag = sb("diag", [128, GB])
        spare = pairs[:, :, :, :].rearrange("p c k n -> p (c k n)")
        w1_sb = spare[:, 0:FIELDS * CIN].rearrange("p (m o) -> p m o", m=FIELDS)
        g_high = sb_over("g_high", pairs_at + 4 * 2 * KT * COLS, [CIN, L2_SPLIT, BATCH], fp32r)
        g_low = sb_over("g_low", g_at, [CIN, FIELDS + 1, BATCH], fp32r)
        w1_high = sb_over("w1_high", periodic_at, [CIN, L2_SPLIT, CIN], fp32r)
        w1_low = sb_over("w1_low", pairs_at, [CIN, FIELDS, CIN], fp32r)
        wt1_at = FIELDS * CIN
        wt1_sb = spare[:, wt1_at:wt1_at + 2 * H1].rearrange("p (k j) -> p k j", k=2)
        wt2_at = wt1_at + 2 * H1
        wt2_sb = spare[:, wt2_at:wt2_at + H1T * H2].rearrange("p (k j) -> p k j", k=H1T)
        mlp_size = 2 * H1 + H1T * H2
        mlp_w = spare[:, wt1_at:wt1_at + mlp_size]
        mlp_low = sb_over("mlp_low", pairs_at + 4 * wt1_at, [128, mlp_size], fp32r)
        mlp_high = sb_over("mlp_high", emb_at, [128, mlp_size], fp32r)
        wt1_low, wt1_high = (w[:, 0:2 * H1].rearrange("p (k j) -> p k j", k=2) for w in (mlp_low, mlp_high))
        wt2_low, wt2_high = (w[:, 2 * H1:].rearrange("p (k j) -> p k j", k=H1T) for w in (mlp_low, mlp_high))
        h1_low, h1_high = g_low[:, 0:H1T, :], g_low[:, H1T:2 * H1T, :]
        sum_low = [g_low[:, FIELDS, :], g_low[:, 2 * H1T, :]]
        sum_high = [g_low[:, 2 * H1T + 1, :], g_low[:, 2 * H1T + 2, :]]
        h2 = g_sb[:, 2 * H1T + 3:2 * H1T + 3 + H2T, :]
        stage = g_sb[:, :, :].rearrange("p m b -> p (m b)")
        w0_stage = stage[0:ROWS, 0:2 * KT * CIN]
        at = 2 * KT * CIN
        table = stage[:, at:at + TABLE_ROWS * DIM].rearrange("p (r d) -> p r d", d=DIM)
        at += TABLE_ROWS * DIM
        size = TABLE_ROWS * DIM * PARTS // 2
        parts = stage[:, at:at + size].bitcast(bf16).rearrange("p (r n d) -> p r n d", n=PARTS, d=DIM)
        at += size
        last_slot = (CHUNKS - 1) * KT * COLS
        ids_all = [stage[:, at:at + SMALL * TILE].bitcast(i32),
                   spare[:, last_slot:last_slot + SMALL * TILE].bitcast(i32)]
        at += SMALL * TILE
        ids_16 = []
        for t in range(ONE_HOT_TILES):
            ids_16.append(stage[:, at:at + SMALL * TILE // 2].bitcast(fp16))
            at += SMALL * TILE // 2
        rest = stage[:, at:at + TABLE_ROWS * DIM].rearrange("p (r d) -> p r d", d=DIM)

        def one_hots(memory, at, v, fields):
            n = ROWS_EACH[v] * fields * TILE // 2
            return memory[:, at:at + n].bitcast(bf16).rearrange("p (r f b) -> p r f b", r=ROWS_EACH[v], b=TILE)

        table_end = VOCAB_ROWS[0].stop * TILE // 2
        one_hot = [[one_hots(spare, 0, 0, OF_VOCAB[0]), one_hots(spare, table_end, 1, OF_VOCAB[1])],
                   [one_hots(stage, at, 0, OF_VOCAB[0]),
                    one_hots(spare, CHUNKS * KT * COLS - OF_VOCAB[1] * ROWS_EACH[1] * TILE // 2, 1, OF_VOCAB[1])]]
        at += table_end
        wt1_ctx = stage[0:CTX, at:at + H1]
        ctx_sb = x1[0:CTX, 0, :, :].rearrange("p b d -> p (b d)")
        row_of = sb("row_of", [128, len(SMALL_VOCABS), max(ROWS_EACH)])

        bank = [ctx.enter_context(nc.psum_tensor(f"bank{i}", [128, 512], fp32)) for i in range(8)]
        ps_in, ps_x1, ps_x1t, ps_x0t = bank[0:4], bank[4:6], bank[6], bank[7]
        ps_g = ps_in
        ps_picked = [ps_in[0], ps_in[1], ps_x1[0], ps_x1[1]]
        ps_ctx = [ps_in[2], ps_in[3], ps_x1t, ps_x0t]
        ps_l2, ps_h1, ps_h2, ps_y = ps_x1t, [ps_x1[0], ps_x1[1], ps_x0t, ps_in[0]], ps_in[1:3], ps_in[3]

        s_ids = sem("s_ids")
        s_small_ids = sem("s_small_ids")
        s_tables = sems("s_tables", len(SMALL_VOCABS))
        s_next_ids = sem("s_next_ids")
        s_ids_16 = sem("s_ids_16")
        s_parts = sems("s_parts", len(SMALL_VOCABS))
        s_one_hot = [sems(f"s_one_hot{t}_", len(SMALL_VOCABS)) for t in range(ONE_HOT_TILES)]
        s_picked = sems("s_picked", len(PICKED))
        s_small = sem("s_small")
        s_ones = sem("s_ones")
        s_rows = sems("s_rows", TILES)
        s_late_rows = sems("s_late_rows", TILES)
        s_gathered, s_gathered_late = sem("s_gathered"), sem("s_gathered_late")
        s_consts = sem("s_consts")
        s_w0 = sem("s_w0")
        s_w1, s_mlp = sem("s_w1"), sem("s_mlp")
        s_ctx = sem("s_ctx")
        s_ctx_mm, s_ctx_part = sem("s_ctx_mm"), sem("s_ctx_part")
        s_w0_sum = sem("s_w0_sum")
        s_wrap = sem("s_wrap")
        s_in_t = sems("s_in_t", QUARTERS)
        s_periodic = sems("s_periodic", QUARTERS)
        s_left = sems("s_left", CHUNKS)
        s_shift = [sems(f"s_shift{c}_", KT) for c in range(CHUNKS)]
        s_z = sems("s_z", CHUNKS)
        s_z_high = sem("s_z_high")
        s_z_low = sems("s_z_low", CHUNKS)
        s_w0_high = sem("s_w0_high")
        s_l1 = sems("s_l1", CHUNKS)
        s_x1 = sems("s_x1", 2)
        s_xt = sem("s_xt")
        s_x1_t = sem("s_x1_t")
        s_diag = sem("s_diag")
        s_g = sems("s_g", GROUPS)
        s_g_sb = sems("s_g_sb", GROUPS)
        s_w1_high, s_w1_low, s_g_high, s_g_low = sem("s_w1_high"), sem("s_w1_low"), sem("s_g_high"), sem("s_g_low")
        s_l2_whole = sem("s_l2_whole")
        s_mlp_high, s_mlp_low = sem("s_mlp_high"), sem("s_mlp_low")
        s_l2 = sem("s_l2")
        s_sum_high, s_sum_low = sem("s_sum_high"), sem("s_sum_low")
        s_h1, s_h1_sum = sem("s_h1"), sem("s_h1_sum")
        s_h1_high, s_h1_low = sem("s_h1_high"), sem("s_h1_low")
        s_h2, s_h2_sb = sem("s_h2"), sem("s_h2_sb")
        s_y, s_y_sb, s_out = sem("s_y"), sem("s_y_sb"), sem("s_out")

        block = ctx.enter_context(nc.Block())


        def rows_of(k):
            return ROWS if k < KT - 1 else LAST_ROWS

        def before(t, c):
            return 2 * t + c // 2

        def gathered_from(t):
            return SMALL if t < ONE_HOT_TILES else 0

        @block.sync
        def _(sp):
            sp.dma_start(ids_sb[:, :, :], ids.rearrange("(t p) f -> p t f", p=TILE)).then_inc(s_ids, 16)
            sp.dma_start(row_of[:, :, :], row_ids).then_inc(s_small_ids, 16)
            mine = SMALL * TILE
            sp.dma_start(ids_all[0], small_ids[:, 0:mine].broadcast_to([128, mine])).then_inc(s_small_ids, 16)
            table_src = small_tables.rearrange("p (r d) -> p r d", d=DIM)
            for v, rows in enumerate(VOCAB_ROWS):
                sp.dma_start(table[:, rows, :], table_src[:, rows, :]).then_inc(s_tables[v], 16)
            sp.dma_start(ids_all[1], small_ids[:, mine:].broadcast_to([128, mine])).then_inc(s_next_ids, 16)
            sp.dma_start(ctx_sb, ctx_t).then_inc(s_ctx, 16)
            sp.dma_start(wt1_ctx, wt1[2 * CIN:, :]).then_inc(s_ctx, 16)
            sp.dma_start(ident[:, :], ident_c).then_inc(s_consts, 16)
            sp.dma_start(diag[:, :], diag_c).then_inc(s_consts, 16)
            half = KT * CIN
            sp.dma_start(w0_stage[:, 0:half], w0_pq).then_inc(s_w0, 16)
            sp.dma_start(w0_stage[:, half:2 * half], w0_qp).then_inc(s_w0, 16)

            def replicas(t, first):
                transposed = 1 if first else sp.to_reg(t + 1)
                used = None if first else sp.to_reg(t)
                read = [None if first else sp.to_reg(CHUNKS * (t - 1) + c + 1) for c in range(CHUNKS)]
                for c in range(CHUNKS):
                    if c == 0:
                        for q in range(QUARTERS):
                            sp.wait_ge(s_periodic[q], transposed)
                    if not first:
                        sp.wait_ge(s_xt, read[c])
                    for j in range(SHIFTS):
                        start = (FIELDS - KT * j) % FIELDS
                        sp.dma_start(left[j * FIELDS:(j + 1) * FIELDS, c, :, :],
                                     periodic[start:start + FIELDS, c, :, :]).then_inc(s_left[c], 16)
                    if not first:
                        sp.wait_ge(s_l1[c], used)
                    elif c == 2:
                        sp.wait_ge(s_picked[3], 1)
                    for k in range(1, KT):
                        rows = rows_of(k)
                        src = periodic[k:k + rows, c, :, :].rearrange("p b d -> p (b d)")
                        sp.dma_start(pairs[0:rows, c, k, :], src).then_inc(s_shift[c][k], 16)

            replicas(0, True)
            with sp.Fori(1, TILES) as t:
                replicas(t, False)
            w1_src = w1.rearrange("(m n) o -> n m o", n=CIN)
            sp.wait_ge(s_l1[0], TILES)
            sp.dma_start(w1_sb[:, 0:W1_FIRST, :], w1_src[:, 0:W1_FIRST, :]).then_inc(s_w1, 16)
            sp.wait_ge(s_l1[1], TILES)
            sp.dma_start(w1_sb[:, W1_FIRST:, :], w1_src[:, W1_FIRST:, :]).then_inc(s_w1, 16)
            sp.dma_start(wt1_sb, wt1[0:2 * CIN, :].rearrange("(k p) j -> p k j", p=CIN)).then_inc(s_mlp, 16)
            sp.dma_start(wt2_sb, wt2.rearrange("(k p) j -> p k j", p=128)).then_inc(s_mlp, 16)
            sp.dma_start(wt3_sb[:, :], wt3).then_inc(s_mlp, 16)
            sp.dma_start(bt1_sb[:, :], bt1).then_inc(s_mlp, 16)
            sp.dma_start(bt2_sb[:, :], bt2).then_inc(s_mlp, 16)
            sp.wait_ge(s_y_sb, 1)
            sp.dma_start(out.rearrange("b o -> o b"), y_sb).then_inc(s_out, 16)
            sp.wait_ge(s_out, 16)

        @block.gpsimd
        def _(pool):
            pool.wait_ge(s_ids, 16)
            for t in range(TILES):
                for f in range(gathered_from(t), FIELDS):
                    pool.indirect_dma_start(
                        out=emb[:, t, f, :], out_offset=None, in_=tables[f],
                        in_offset=bass.IndirectOffsetOnAxis(ap=ids_sb[:, t, f:f + 1], axis=0),
                    ).then_inc(s_rows[t] if f < LATE else s_late_rows[t], 16)
                    if t >= 2 and f == 3:
                        pool.wait_ge(s_late_rows[t - 1], 16 * (FIELDS - LATE))
                        pool.sem_inc(s_gathered_late, 1)
                    if t >= 1 and f == LATE + 3:
                        pool.wait_ge(s_rows[t], 16 * (LATE - gathered_from(t)))
                        pool.sem_inc(s_gathered, 1)
            pool.wait_ge(s_late_rows[TILES - 1], 16 * (FIELDS - LATE))
            pool.sem_inc(s_gathered_late, 1)

        @block.vector
        def _(dve):
            def wrap_first():
                src = emb[:, 0, :, :]
                dve.wait_ge(s_small, 2)
                for r in range(0, PERIODIC, FIELDS):
                    n = min(SMALL, PERIODIC - r)
                    nc.vector.tensor_copy(emb_wrap[:, r:r + n, :], src[:, 0:n, :]).then_inc(s_wrap, 1)
                dve.wait_ge(s_rows[0], 16 * (LATE - SMALL))
                dve.wait_ge(s_late_rows[0], 16 * (FIELDS - LATE))
                for r in range(0, ROWS, FIELDS):
                    nc.vector.tensor_copy(emb_wrap[:, r + SMALL:r + FIELDS, :], src[:, SMALL:, :]).then_inc(s_wrap, 1)

            def wrap_late(t):
                dve.wait_ge(s_gathered_late, t)
                dve.wait_ge(s_wrap, WRAPS * t + 4)
                for r in range(0, ROWS, FIELDS):
                    nc.vector.tensor_copy(
                        emb_wrap[:, r + LATE:r + FIELDS, :],
                        emb[:, bass.ds(t, 1), LATE:, :].rearrange("p a f d -> p (a f) d")).then_inc(s_wrap, 1)

            def products(t, c, first, tiles=range(KT)):
                for k in tiles:
                    a = left[0:rows_of(k), c, :, :].rearrange("p b d -> p (b d)")
                    z = b = pairs[0:rows_of(k), c, k, :]
                    if k == 0:
                        dve.wait_ge(s_left[c], 16 * SHIFTS * (t + 1))
                        if not first:
                            dve.wait_ge(s_l1[c], t)
                        b = periodic[0:ROWS, c, :, :].rearrange("p b d -> p (b d)")
                    else:
                        dve.wait_ge(s_shift[c][k], 16 * (t + 1))
                    nc.vector.tensor_tensor(z, b, a, ALU.mult).then_inc(s_z[c], 1)

            def low_parts(t, c):
                for i, k in enumerate(SPLIT):
                    dve.wait_ge(s_z_high, len(SPLIT) * (CHUNKS * t + c) + i + 1)
                    nc.vector.tensor_tensor(z_low[0:ROWS, c, k, :], pairs[0:ROWS, c, k, :],
                                            z_high[:, i, :].bitcast(fp32), ALU.subtract).then_inc(s_z_low[c], 1)

            def diagonal(t, c, first):
                n = CHUNKS * t + c
                dve.wait_ge(s_xt, n + 1)
                if not first or c >= 2:
                    for g in range(GROUPS):
                        dve.wait_ge(s_g[g], n - 1)
                src = ps_x0t[:, 0:GROUPS * FIELDS].rearrange("p (g m) -> p g m", g=GROUPS)
                nc.vector.tensor_tensor(
                    x0_diag[:, c % 2, :, 0:FIELDS, :],
                    src[:, :, :, None].broadcast_to([128, GROUPS, FIELDS, GB]),
                    diag[:, None, None, :].broadcast_to([128, GROUPS, FIELDS, GB]), ALU.mult).then_inc(s_diag, 1)

            dve.wait_ge(s_small_ids, 32)
            nc.vector.tensor_copy(ids_16[0], ids_all[0]).then_inc(s_ids_16, 1)
            dve.wait_ge(s_ids_16, 1)

            def compares(t, v):
                n = OF_VOCAB[v]
                f0 = v * OF_VOCAB[0]
                for r in range(ROWS_EACH[v]):
                    nc.vector.tensor_scalar(
                        one_hot[t][v][:, r, :, :].rearrange("p f b -> p (f b)"),
                        ids_16[t][:, f0 * TILE:(f0 + n) * TILE], row_of[:, v, r:r + 1], None,
                        ALU.is_equal).then_inc(s_one_hot[t][v], 1)

            def subtract_part(v, n):
                rows = VOCAB_ROWS[v]
                src = (table, rest)[n][:, rows, :]
                dst = rest[:, rows, :] if n == 0 else parts[:, rows, 2, :]
                dve.wait_ge(s_parts[v], 2 * n + 1)
                nc.vector.tensor_tensor(dst, src, parts[:, rows, n, :], ALU.subtract).then_inc(s_parts[v], 1)

            def sum_parts(q):
                dve.wait_ge(s_picked[q], 1)
                t, f0, f1 = PICKED[q]
                nc.vector.tensor_reduce(
                    emb[:, t, f0:f1, :],
                    ps_picked[q][:, 0:(f1 - f0) * PARTS * DIM].rearrange("p (f n d) -> p f d n", n=PARTS, d=DIM),
                    axis=AX.X, op=ALU.add).then_inc(s_small, 1)

            compares(0, 0)
            subtract_part(0, 0)
            subtract_part(1, 0)
            subtract_part(0, 1)
            compares(0, 1)
            subtract_part(1, 1)
            sum_parts(0)
            dve.wait_ge(s_w0, 32)
            half = KT * CIN
            nc.vector.tensor_tensor(w0_sb[:, :, :].rearrange("p k o -> p (k o)"), w0_stage[:, 0:half],
                                    w0_stage[:, half:2 * half], ALU.add).then_inc(s_w0_sum, 1)
            dve.wait_ge(s_consts, 32)
            for s in range(2):
                nc.vector.tensor_copy(x0_diag[:, s, :, FIELDS, :],
                                      diag[:, None, :].broadcast_to([128, GROUPS, GB])).then_inc(s_ones, 1)
            sum_parts(1)
            wrap_first()
            dve.wait_ge(s_ids_16, 2)
            for v in range(2):
                dve.wait_ge(s_parts[v], 4)
            compares(1, 0)
            compares(1, 1)
            sum_parts(2)

            def tile(t, first=False, last=False):
                if first:
                    low_parts(t, 1)
                    products(t, 2, first)
                    low_parts(t, 2)
                    diagonal(t, 0, first)
                    wrap_late(1)
                    products(t, 3, first)
                else:
                    low_parts(t, 0)
                    products(t, 1, first, range(4, KT))
                    products(t, 2, first, range(5))
                    low_parts(t, 1)
                    products(t, 2, first, range(5, KT))
                    diagonal(t, 0, first)
                    low_parts(t, 2)
                    products(t, 3, first)
                if not first and not last:
                    wrap_late(t + 1)
                diagonal(t, 1, first)
                low_parts(t, 3)
                if not last:
                    products(t + 1, 0, False, range(2))
                diagonal(t, 2, first)
                if not last:
                    products(t + 1, 0, False, range(2, 4))
                diagonal(t, 3, first)
                if not last:
                    products(t + 1, 0, False, range(4, KT))
                    products(t + 1, 1, False, range(4))

            products(0, 0, True)
            dve.wait_ge(s_w0_high, 1)
            nc.vector.tensor_tensor(w0_low[:, SPLIT[0]:SPLIT[-1] + 1, :], w0_sb[:, SPLIT[0]:SPLIT[-1] + 1, :],
                                    w0_high[:, :, :].bitcast(fp32), ALU.subtract).then_inc(s_w0_sum, 1)
            low_parts(0, 0)
            products(0, 1, True, range(3))
            sum_parts(3)
            products(0, 1, True, range(3, KT))
            tile(0, first=True)
            with dve.Fori(1, TILES - 1) as t:
                tile(t)
            tile(TILES - 1, last=True)

            dve.wait_ge(s_w1_high, 1)
            nc.vector.tensor_tensor(w1_low[:, L2_WHOLE:, :], w1_sb[:, L2_WHOLE:, :], w1_high[:, :, :].bitcast(fp32),
                                    ALU.subtract).then_inc(s_w1_low, 1)
            for i, m in enumerate(range(L2_WHOLE, FIELDS)):
                dve.wait_ge(s_g_high, i + 1)
                nc.vector.tensor_tensor(g_low[:, m, :], g_sb[:, m, :], g_high[:, i, :].bitcast(fp32),
                                        ALU.subtract).then_inc(s_g_low, 1)
            dve.wait_ge(s_mlp_high, 1)
            nc.vector.tensor_tensor(mlp_low[:, :], mlp_w, mlp_high[:, :].bitcast(fp32),
                                    ALU.subtract).then_inc(s_mlp_low, 1)
            for n, src in enumerate((sum1, ps_l2[:, :])):
                dve.wait_ge(s_sum_high, n + 1)
                nc.vector.tensor_tensor(sum_low[n], src, sum_high[n].bitcast(fp32),
                                        ALU.subtract).then_inc(s_sum_low, 1)

            def h1_sum(j):
                dve.wait_ge(s_h1, j + 1)
                nc.vector.scalar_tensor_tensor(ctx_part[:, j, :], ps_h1[j][:, :], bt1_sb[:, j:j + 1], ctx_part[:, j, :],
                                               ALU.add, ALU.add).then_inc(s_h1_sum, 1)

            h1_sum(0)
            for j in range(H1T):
                if j + 1 < H1T:
                    h1_sum(j + 1)
                dve.wait_ge(s_h1_high, j + 1)
                nc.vector.scalar_tensor_tensor(h1_low[:, j, :], ctx_part[:, j, :], 0.0, h1_high[:, j, :].bitcast(fp32),
                                               ALU.max, ALU.subtract).then_inc(s_h1_low, 1)

        @block.scalar
        def _(act):
            def wrap(t):
                act.wait_ge(s_small, 4)
                act.wait_ge(s_gathered, t)
                for q in range(QUARTERS):
                    act.wait_ge(s_in_t[q], t)
                src = emb[:, bass.ds(t, 1), :, :].rearrange("p a f d -> p (a f) d")
                for r in range(0, PERIODIC, FIELDS):
                    n = min(LATE, PERIODIC - r)
                    nc.scalar.copy(emb_wrap[:, r:r + n, :], src[:, 0:n, :]).then_inc(s_wrap, 1)

            def periodic_copy(t, q, first):
                act.wait_ge(s_in_t[q], t + 1)
                if q == 0 and not first:
                    for c in range(CHUNKS):
                        act.wait_ge(s_z[c], KT * t)
                dst = periodic[:, :, :, 4 * q:4 * q + 4].rearrange("p c b d -> p d (c b)")
                src = ps_in[q][0:PERIODIC, :].rearrange("p (d b) -> p d b", d=4)
                nc.scalar.copy(dst, src).then_inc(s_periodic[q], 1)

            def high_parts(t, c, first):
                for i, k in enumerate(SPLIT):
                    act.wait_ge(s_z[c], KT * t + k + 1)
                    if i == 0 and c > 0:
                        act.wait_ge(s_l1[c - 1], t + 1)
                    elif i == 0 and not first:
                        act.wait_ge(s_l1[CHUNKS - 1], t)
                    nc.scalar.copy(z_high[:, i, :], pairs[0:ROWS, c, k, :]).then_inc(s_z_high, 1)

            def x1_copy(t, c, first):
                s, n = c % 2, CHUNKS * t + c
                act.wait_ge(s_l1[c], t + 1)
                if not first or c >= 2:
                    act.wait_ge(s_xt, n - 1)
                nc.scalar.copy(x1[:, s, :, :].rearrange("p b d -> p (b d)"), ps_x1[s][:, :]).then_inc(s_x1[s], 1)

            def x1_t_copy(t, c, first):
                n = CHUNKS * t + c
                act.wait_ge(s_xt, n + 1)
                if not first or c >= 2:
                    for g in range(GROUPS):
                        act.wait_ge(s_g[g], n - 1)
                nc.scalar.copy(x1_t[:, c % 2, :, :].rearrange("p g n -> p (g n)"), ps_x1t[:, :]).then_inc(s_x1_t, 1)

            def g_copy(t, c):
                for g in range(GROUPS):
                    act.wait_ge(s_g[g], CHUNKS * t + c + 1)
                    col = t * TILE + c * CB + g * GB
                    nc.scalar.copy(g_sb[:, :, bass.ds(col, GB)],
                                   ps_g[g][:, 0:(FIELDS + 1) * GB].rearrange("p (m b) -> p m b", b=GB)
                                   ).then_inc(s_g_sb[g], 1)

            for n, src in enumerate((table, rest)):
                for v, rows in enumerate(VOCAB_ROWS):
                    if n == 0:
                        act.wait_ge(s_tables[v], 16)
                    else:
                        act.wait_ge(s_parts[v], 2)
                    nc.scalar.copy(parts[:, rows, n, :], src[:, rows, :]).then_inc(s_parts[v], 1)
            act.wait_ge(s_next_ids, 16)
            nc.scalar.copy(ids_16[1], ids_all[1]).then_inc(s_ids_16, 1)
            for j in range(H1T):
                if j == 2:
                    act.wait_ge(s_w0_sum, 1)
                    nc.scalar.copy(w0_high[:, :, :], w0_sb[:, SPLIT[0]:SPLIT[-1] + 1, :]).then_inc(s_w0_high, 1)
                act.wait_ge(s_ctx_mm, j + 1)
                nc.scalar.copy(ctx_part[:, j, :], ps_ctx[j][:, :]).then_inc(s_ctx_part, 1)
            for q in range(QUARTERS):
                periodic_copy(0, q, True)
            act.wait_ge(s_w0_sum, 1)

            def tile(t, first=False, last=False):
                high_parts(t, 0, first)
                high_parts(t, 1, first)
                x1_copy(t, 0, first)
                high_parts(t, 2, first)
                x1_copy(t, 1, first)
                x1_t_copy(t, 0, first)
                if not last:
                    wrap(t + 1)
                x1_copy(t, 2, first)
                x1_t_copy(t, 1, first)
                g_copy(t, 0)
                if not last:
                    for q in range(QUARTERS):
                        periodic_copy(t + 1, q, False)
                high_parts(t, 3, first)
                x1_copy(t, 3, first)
                x1_t_copy(t, 2, first)
                g_copy(t, 1)
                x1_t_copy(t, 3, first)
                g_copy(t, 2)
                g_copy(t, 3)

            tile(0, first=True)
            with act.Fori(1, TILES - 1) as t:
                tile(t)
            tile(TILES - 1, last=True)

            act.wait_ge(s_w1, 32)
            for c in range(CHUNKS):
                act.wait_ge(s_z[c], KT * TILES)
            nc.scalar.copy(w1_high[:, :, :], w1_sb[:, L2_WHOLE:, :]).then_inc(s_w1_high, 1)
            for g in range(GROUPS):
                act.wait_ge(s_g_sb[g], CHUNKS * TILES)
            for i, m in enumerate(range(L2_WHOLE, FIELDS)):
                nc.scalar.copy(g_high[:, i, :], g_sb[:, m, :]).then_inc(s_g_high, 1)
            act.wait_ge(s_mlp, 16 * 5)
            act.wait_ge(s_wrap, WRAPS * TILES)
            nc.scalar.copy(mlp_high[:, :], mlp_w).then_inc(s_mlp_high, 1)
            act.wait_ge(s_l2_whole, 1)
            nc.scalar.copy(sum_high[0], sum1).then_inc(s_sum_high, 1)
            act.wait_ge(s_l2, 1)
            nc.scalar.copy(sum_high[1], ps_l2[:, :]).then_inc(s_sum_high, 1)
            for j in range(H1T):
                act.wait_ge(s_h1_sum, j + 1)
                nc.scalar.activation(h1_high[:, j, :], ctx_part[:, j, :], ACT.Relu).then_inc(s_h1_high, 1)
            for j in range(H2T):
                act.wait_ge(s_h2, j + 1)
                nc.scalar.activation(h2[:, j, :], ps_h2[j][:, :], ACT.Relu,
                                     bias=bt2_sb[:, j:j + 1]).then_inc(s_h2_sb, 1)
            act.wait_ge(s_y, 1)
            nc.scalar.copy(y_sb, ps_y[0:1, :]).then_inc(s_y_sb, 1)

        @block.tensor
        def _(pe):
            def inputs_t(t, first):
                pe.wait_ge(s_wrap, WRAPS * (t + 1))
                for q in range(QUARTERS):
                    if not first:
                        pe.wait_ge(s_g_sb[q], CHUNKS * (t - 1) + 1)
                    for i in range(4):
                        last = nc.tensor.transpose(ps_in[q][0:PERIODIC, i * TILE:(i + 1) * TILE],
                                                   emb_wrap[:, :, 4 * q + i], ident[:, :])
                    last.then_inc(s_in_t[q], 1)

            def layer1_whole(t, c, first):
                s = c % 2
                if not first or c >= 2:
                    pe.wait_ge(s_x1[s], before(t, c))
                for k in WHOLE:
                    rows = rows_of(k)
                    pe.wait_ge(s_z[c], KT * t + k + 1)
                    nc.tensor.matmul(ps_x1[s][:, :], w0_sb[0:rows, k, :], pairs[0:rows, c, k, :],
                                     start=k == WHOLE[0], stop=False)

            def layer1_split(t, c):
                out = ps_x1[c % 2][:, :]
                for i, k in enumerate(SPLIT):
                    pe.wait_ge(s_z_low[c], len(SPLIT) * t + i + 1)
                    w_high, w_low = w0_high[:, i, :], w0_low[:, k, :]
                    high, low = z_high[:, i, :], z_low[0:ROWS, c, k, :]
                    nc.tensor.matmul(out, w_low, high, start=False, stop=False)
                    nc.tensor.matmul(out, w_high, low, start=False, stop=False)
                    last = nc.tensor.matmul(out, w_high, high, start=False, stop=k == SPLIT[-1])
                last.then_inc(s_l1[c], 1)

            def layer1(t, c, first):
                layer1_whole(t, c, first)
                layer1_split(t, c)

            def chunk_t(t, c, first):
                n = CHUNKS * t + c
                pe.wait_ge(s_x1[c % 2], before(t, c) + 1)
                if not first or c >= 1:
                    pe.wait_ge(s_x1_t, n)
                    pe.wait_ge(s_diag, n)
                for g in range(GROUPS):
                    rows = slice(g * GB, (g + 1) * GB)
                    nc.tensor.transpose(ps_x1t[:, g * CIN:(g + 1) * CIN],
                                        x1[:, c % 2, rows, :].rearrange("p b d -> p (b d)"), ident[:, :])
                for g in range(GROUPS):
                    rows = slice(g * GB, (g + 1) * GB)
                    last = nc.tensor.transpose(ps_x0t[:, g * FIELDS:(g + 1) * FIELDS],
                                               left[0:FIELDS, c, rows, :].rearrange("p b d -> p (b d)"),
                                               ident[0:FIELDS, 0:FIELDS])
                last.then_inc(s_xt, 1)

            def g_products(t, c, first, last=False):
                n = CHUNKS * t + c
                pe.wait_ge(s_x1_t, n + 1)
                pe.wait_ge(s_diag, n + 1)
                for g in range(GROUPS):
                    if not first or c >= 1:
                        pe.wait_ge(s_g_sb[g], n)
                    pe.wait_ge(s_periodic[g], t + 1 if c == 0 or last else t + 2)
                    nc.tensor.matmul(ps_g[g][:, 0:(FIELDS + 1) * GB], x1_t[:, c % 2, g, :],
                                     x0_diag[:, c % 2, g, :, :].rearrange("p m b -> p (m b)"),
                                     start=True, stop=True).then_inc(s_g[g], 1)

            def pick(t, v):
                f0, rows = v * OF_VOCAB[0], ROWS_EACH[v]
                pe.wait_ge(s_one_hot[t][v], rows)
                pe.wait_ge(s_parts[v], 4)
                for i in range(OF_VOCAB[v]):
                    q = [q for q, (tile, first, end) in enumerate(PICKED) if tile == t and first <= f0 + i < end][0]
                    at = (f0 + i - PICKED[q][1]) * PARTS * DIM
                    for r in range(rows):
                        table_row = parts[:, VOCAB_ROWS[v].start + i * rows + r, :, :]
                        last = nc.tensor.matmul(ps_picked[q][:, at:at + PARTS * DIM], one_hot[t][v][:, r, i, :],
                                                table_row.rearrange("p n d -> p (n d)"),
                                                start=r == 0, stop=r == rows - 1)
                    if f0 + i + 1 == PICKED[q][2]:
                        last.then_inc(s_picked[q], 1)

            for v in range(2):
                pick(0, v)
                if v == 0:
                    pe.wait_ge(s_ctx, 32)
                for j in (2 * v, 2 * v + 1):
                    nc.tensor.matmul(ps_ctx[j][:, :], wt1_ctx[:, j * 128:(j + 1) * 128], ctx_sb,
                                     start=True, stop=True).then_inc(s_ctx_mm, 1)
            pe.wait_ge(s_consts, 32)
            pe.wait_ge(s_ctx_part, 2)
            inputs_t(0, True)
            pick(1, 0)
            pe.wait_ge(s_w0_sum, 1)
            pe.wait_ge(s_ones, 2)
            pe.wait_ge(s_ctx_part, H1T)
            pe.wait_ge(s_small, 3)

            def tile(t, first=False, last=False):
                layer1_whole(t, 0, first)
                if first:
                    pick(1, 1)
                    pe.wait_ge(s_w0_sum, 2)
                layer1_split(t, 0)
                if first:
                    pe.wait_ge(s_small, 4)
                layer1(t, 1, first)
                chunk_t(t, 0, first)
                layer1(t, 2, first)
                chunk_t(t, 1, first)
                g_products(t, 0, first)
                if not last:
                    inputs_t(t + 1, False)
                layer1(t, 3, first)
                chunk_t(t, 2, first)
                g_products(t, 1, first, last)
                chunk_t(t, 3, first)
                g_products(t, 2, first, last)
                g_products(t, 3, first, last)

            tile(0, first=True)
            with pe.Fori(1, TILES - 1) as t:
                tile(t)
            tile(TILES - 1, last=True)

            pe.wait_ge(s_w1, 32)
            before_last = slice(0, (TILES - 1) * TILE)
            last_tile = slice((TILES - 1) * TILE, BATCH)
            for g in range(GROUPS):
                pe.wait_ge(s_g_sb[g], CHUNKS * (TILES - 1))
            nc.tensor.matmul(ps_l2[:, before_last], w1_sb[:, 0, :], g_sb[:, 0, before_last], start=True, stop=False)
            for g in range(GROUPS):
                pe.wait_ge(s_g_sb[g], CHUNKS * TILES)
            nc.tensor.matmul(ps_l2[:, last_tile], w1_sb[:, 0, :], g_sb[:, 0, last_tile], start=False, stop=False)
            for m in range(1, L2_WHOLE):
                last = nc.tensor.matmul(ps_l2[:, :], w1_sb[:, m, :], g_sb[:, m, :], start=False, stop=False)
            last.then_inc(s_l2_whole, 1)
            pe.wait_ge(s_w1_low, 1)
            for i, m in enumerate(range(L2_WHOLE, FIELDS)):
                pe.wait_ge(s_g_low, i + 1)
                nc.tensor.matmul(ps_l2[:, :], w1_low[:, m, :], g_high[:, i, :], start=False, stop=False)
                nc.tensor.matmul(ps_l2[:, :], w1_high[:, i, :], g_low[:, m, :], start=False, stop=False)
                last = nc.tensor.matmul(ps_l2[:, :], w1_high[:, i, :], g_high[:, i, :],
                                        start=False, stop=m == FIELDS - 1)
            last.then_inc(s_l2, 1)
            pe.wait_ge(s_mlp_low, 1)
            for n in range(2):
                pe.wait_ge(s_sum_low, n + 1)
                for j in range(H1T):
                    high, low = (w[:, n, j * 128:(j + 1) * 128] for w in (wt1_high, wt1_low))
                    nc.tensor.matmul(ps_h1[j][:, :], low, sum_high[n], start=n == 0, stop=False)
                    nc.tensor.matmul(ps_h1[j][:, :], high, sum_low[n], start=False, stop=False)
                    last = nc.tensor.matmul(ps_h1[j][:, :], high, sum_high[n], start=False, stop=n == 1)
                    if n == 1:
                        last.then_inc(s_h1, 1)
            for k in range(H1T):
                pe.wait_ge(s_h1_low, k + 1)
                for j in range(H2T):
                    high, low = (w[:, k, j * 128:(j + 1) * 128] for w in (wt2_high, wt2_low))
                    nc.tensor.matmul(ps_h2[j][:, :], low, h1_high[:, k, :], start=k == 0, stop=False)
                    nc.tensor.matmul(ps_h2[j][:, :], high, h1_low[:, k, :], start=False, stop=False)
                    last = nc.tensor.matmul(ps_h2[j][:, :], high, h1_high[:, k, :], start=False, stop=k == H1T - 1)
                    if k == H1T - 1:
                        last.then_inc(s_h2, 1)
            for j in range(H2T):
                pe.wait_ge(s_h2_sb, j + 1)
                last = nc.tensor.matmul(ps_y[0:1, :], wt3_sb[:, j:j + 1], h2[:, j, :],
                                        start=j == 0, stop=j == H2T - 1)
            last.then_inc(s_y, 1)


def kernel(**inputs):
    import concourse.bacc as bacc
    from concourse.bass_utils import run_bass_kernel_spmd

    a = {k: np.ascontiguousarray(v) for k, v in inputs.items()}
    order = np.array(ORDER)
    small = [a[f"tbl_{f}"].reshape(SMALL_ROWS, -1) for f in ORDER[:SMALL]]
    small_tables = np.zeros((128, TABLE_ROWS * DIM), np.float32)
    small_tables[:SMALL_ROWS] = np.concatenate(small, axis=1)
    r = np.arange(max(ROWS_EACH))
    row_ids = np.stack([np.arange(128)[:, None] * n + r for n in ROWS_EACH], axis=1).astype(np.float32)
    j, n, k = np.meshgrid(np.arange(SHIFTS), np.arange(FIELDS), np.arange(KT), indexing="ij")
    p, q = (n - KT * j) % FIELDS, (n + k) % FIELDS
    w0 = a["L0_rec_W0"]
    p, q = order[p], order[q]
    w0_pq = w0[p * FIELDS + q].reshape(ROWS, KT * CIN)
    w0_qp = np.where((p != q)[..., None], w0[q * FIELDS + p], np.float32(0)).reshape(ROWS, KT * CIN)
    arrays = {f"tbl_{f}": a[f"tbl_{f}"] for f in range(FIELDS)}
    w1 = a["L0_rec_W1"].reshape(FIELDS, CIN, CIN)[order].reshape(FIELDS * CIN, CIN)
    ids = np.ascontiguousarray(a["ids"][:, order])
    arrays |= {
        "ids": ids, "small_ids": ids[:ONE_HOT_TILES * TILE, :SMALL].reshape(ONE_HOT_TILES, TILE, SMALL)
                                 .transpose(0, 2, 1).reshape(1, -1),
        "small_tables": small_tables, "row_ids": row_ids, "ctx_t": np.ascontiguousarray(a["dense_ctx"].T),
        "w0_pq": w0_pq, "w0_qp": w0_qp,
        "w1": w1, "wt1": a["W_top1"], "bt1": np.ascontiguousarray(a["b_top1"].reshape(H1T, 128).T),
        "wt2": a["W_top2"], "bt2": np.ascontiguousarray(a["b_top2"].reshape(H2T, 128).T),
        "wt3": np.ascontiguousarray(a["W_top3"].reshape(H2T, 128).T),
        "ident_c": np.eye(128, dtype=np.float32),
        "diag_c": (np.arange(128)[:, None] // DIM == np.arange(GB)).astype(np.float32),
    }
    nc = bacc.Bacc("TRN2", target_bir_lowering=False, num_devices=1)
    aps = {name: nc.dram_tensor(name, x.shape, mybir.dt.from_np(x.dtype), kind="ExternalInput").ap()
           for name, x in arrays.items()}
    out = nc.dram_tensor("out", (BATCH, 1), mybir.dt.float32, kind="ExternalOutput").ap()
    tables = [aps.pop(f"tbl_{f}") for f in ORDER]
    dlrm_tower(nc, tables, out=out, **aps)
    r = run_bass_kernel_spmd(nc, [arrays], core_ids=[0])
    return r.results[0]["out"]
```
